# Optimizing a Trainium2 kernel written in Bass

```python
import numpy as np
import jax
import jax.numpy as jnp

def _softmax(x, axis=-1):
    return jax.nn.softmax(x, axis=axis)

def _gelu(x):
    return jax.nn.gelu(x, approximate=True)

def _silu(x):
    return jax.nn.silu(x)

def _sigmoid(x):
    return jax.nn.sigmoid(x)

def _layernorm(x, axis=-1, eps=1e-05):
    m = jnp.mean(x, axis=axis, keepdims=True)
    v = jnp.var(x, axis=axis, keepdims=True)
    return (x - m) / jnp.sqrt(v + eps)

def _scatter_add(tgt, idx, src, axis=0):
    return tgt.at[idx].add(src)

def _segment_sum(src, seg, n):
    return jax.ops.segment_sum(src, seg, n)
kernel_name = 'mk_gnn_preln_d2_gnn_r32_42bebf'

def setup_inputs(seed: int=0):
    np.random.seed(seed)
    _w = jnp.asarray

    def _rec_inputs():
        import jax
        import jax.numpy as jnp
        _gk = jax.random.key(seed)
        x = -0.0002117 + 1 * jax.random.normal(jax.random.fold_in(_gk, 1), (3125, 256), jnp.float32)
        src = jax.random.randint(jax.random.fold_in(_gk, 2), (50000,), 0, 3125, jnp.int32)
        dst = jax.random.randint(jax.random.fold_in(_gk, 3), (50000,), 0, 3125, jnp.int32)
        _o = jnp.argsort(dst, stable=True)
        src = src[_o]
        dst = dst[_o]
        edge_type_8 = jax.random.randint(jax.random.fold_in(_gk, 13), (50000,), 0, 8, jnp.int32)
        return (x, src, dst, edge_type_8)
    x, src, dst, edge_type_8 = _rec_inputs()

    def _L0_gnn_setup():
        import jax, jax.numpy as jnp
        import numpy as np
        N = 3125
        E = 50000
        IN = 256
        OUT = 64
        H = 4
        SLOPE = 0.01
        key = jax.random.key(seed)
        k1, k2, k3, k4, k5 = jax.random.split(key, 5)
        h = jax.random.normal(k1, (N, IN), dtype=jnp.float32)
        W = jax.random.normal(k2, (H, OUT, IN), dtype=jnp.float32) * (1.0 / np.sqrt(IN))
        attn = jax.random.normal(k3, (H, 2 * OUT), dtype=jnp.float32) * (1.0 / np.sqrt(2 * OUT))
        edge_src = jax.random.randint(k4, (E,), 0, N, dtype=jnp.int32)
        edge_dst = jax.random.randint(k5, (E,), 0, N, dtype=jnp.int32)
        return {'h': h, 'W': W, 'attn': attn, 'edge_src': edge_src, 'edge_dst': edge_dst}
    _L0_gnn_all = _L0_gnn_setup()
    _L0_gnn_in = {k: v for k, v in _L0_gnn_all.items() if k in ('W', 'attn')}
    del _L0_gnn_all

    def _L1_gnn_setup():
        import jax, jax.numpy as jnp
        import numpy as np
        N_NODES = 50000
        N_EDGES = 25000
        D_IN = 256
        D_OUT = 256
        N_REL = 8
        key = jax.random.key(seed)
        k_x, k_ei, k_et, k_w = jax.random.split(key, 4)
        x = jax.random.normal(k_x, (N_NODES, D_IN), dtype=jnp.float32)
        edge_index = jax.random.randint(k_ei, (2, N_EDGES), 0, N_NODES, dtype=jnp.int32)
        edge_type = jax.random.randint(k_et, (N_EDGES,), 0, N_REL, dtype=jnp.int32)
        limit = float(np.sqrt(6.0 / (D_IN + D_OUT)))
        weight = jax.random.uniform(k_w, (N_REL, D_IN, D_OUT), dtype=jnp.float32, minval=-limit, maxval=limit)
        bias = jnp.zeros((D_OUT,), dtype=jnp.float32)
        return {'x': x, 'edge_index': edge_index, 'edge_type': edge_type, 'weight': weight, 'bias': bias}
    _L1_gnn_all = _L1_gnn_setup()
    _L1_gnn_in = {k: v for k, v in _L1_gnn_all.items() if k in ('weight', 'bias')}
    del _L1_gnn_all
    return {'x': x, 'src': src, 'dst': dst, 'edge_type_8': edge_type_8, 'L0_gnn_W': _L0_gnn_in['W'], 'L0_gnn_attn': _L0_gnn_in['attn'], 'L1_gnn_weight': _L1_gnn_in['weight'], 'L1_gnn_bias': _L1_gnn_in['bias']}

def reference(x, src, dst, edge_type_8, L0_gnn_W, L0_gnn_attn, L1_gnn_weight, L1_gnn_bias):
    import jax
    import jax.numpy as jnp

    def _L0_gnn_ref(h, W, attn, edge_src, edge_dst):
        import jax, jax.numpy as jnp
        import numpy as np
        N = 3125
        E = 50000
        IN = 256
        OUT = 64
        H = 4
        SLOPE = 0.01
        a0 = attn[0]
        a_src, a_dst = (a0[:OUT], a0[OUT:])
        outs = []
        for hd in range(H):
            z = h @ W[hd].T
            s_src = z @ a_src
            s_dst = z @ a_dst
            e = jax.nn.leaky_relu(s_src[edge_src] + s_dst[edge_dst], SLOPE)
            m = jax.ops.segment_max(e, edge_dst, num_segments=N)
            m = jnp.where(jnp.isfinite(m), m, 0.0)
            ex = jnp.exp(e - m[edge_dst])
            den = jax.ops.segment_sum(ex, edge_dst, num_segments=N)
            alpha = ex / jnp.maximum(den[edge_dst], 1e-09)
            msg = alpha[:, None] * z[edge_src]
            outs.append(jax.ops.segment_sum(msg, edge_dst, num_segments=N))
        return jnp.concatenate(outs, axis=1)

    def _L1_gnn_ref(x, edge_index, edge_type, weight, bias):
        import jax, jax.numpy as jnp
        import numpy as np
        N_NODES = 50000
        N_EDGES = 25000
        D_IN = 256
        D_OUT = 256
        N_REL = 8
        num_nodes = x.shape[0]
        row, col = (edge_index[0], edge_index[1])
        xt = jnp.einsum('ni,rio->rno', x, weight)
        messages = xt[edge_type, col]
        out = jax.ops.segment_sum(messages, row, num_segments=num_nodes)
        return jax.nn.relu(out + bias)
    edge_index = jnp.stack([src, dst])
    h = jnp.maximum(_layernorm(x, axis=-1), 0.0)
    x = x + _L0_gnn_ref(h, L0_gnn_W, L0_gnn_attn, src, dst)
    h = jnp.maximum(_layernorm(x, axis=-1), 0.0)
    x = x + _L1_gnn_ref(h, edge_index, edge_type_8, L1_gnn_weight, L1_gnn_bias)
    return x

_drawn_inputs = setup_inputs


def setup_inputs(seed=0):
    import zlib

    import numpy as np

    out = dict(_drawn_inputs(seed))
    spreads = {'L1_gnn_bias': (0.0, 0.331)}
    factors = {}
    for name, (base, spread) in spreads.items():
        noise = np.random.default_rng([zlib.crc32(name.encode()), seed]).standard_normal(out[name].shape)
        drawn = base * np.exp(spread * noise) if base else spread * noise
        out[name] = jnp.asarray(drawn.astype(out[name].dtype))
    for name, factor in factors.items():
        out[name] = (out[name] * factor).astype(out[name].dtype)
    return out
```

```python
import concourse.bass as bass
from concourse import mybir
from contextlib import ExitStack

P = 128
N, E, D = 3125, 50000, 256
H, DH, R = 4, 64, 8
NB = -(-N // P)
EP, EC = 125, 400
NT = EC // 8 * 8 + 16
CH, NCH = 100, 4
ZW = D + 2 * H
MW = D + H
K = 8
NBATCH = NT // K
FC = 5
EPS = 1e-5
SLOPE = 0.01
NO_NODE = -200.0

assert EP * EC == E and CH * NCH == EC and E // P + NB <= NT and NB % FC == 0 and NB % 2 == 1 and NBATCH % 2 == 0


class Chain:

    def __init__(self, eng, sem):
        self.eng, self.sem, self.n, self.off = eng, sem, 0, 0

    def __call__(self, ins):
        ins.then_inc(self.sem, 1)
        self.n += 1
        self.eng.wait_ge(self.sem, self.off + self.n)

    def enter(self, i, per):
        self.off = i * per
        self.start = self.n

    def leave(self, per, trips):
        assert self.n - self.start == per, (self.n - self.start, per)
        self.off = 0
        self.n = self.start + per * trips


def build(nc, x, src, dst, etype, w0, attn, w1, bias, out):
    f32, f16, i32, u16 = mybir.dt.float32, mybir.dt.float16, mybir.dt.int32, mybir.dt.uint16
    ALU, ACT, AX = mybir.AluOpType, mybir.ActivationFunctionType, mybir.AxisListType
    ds = bass.ds

    with ExitStack() as ctx:
        def sb(name, shape, dt=f32):
            return ctx.enter_context(nc.sbuf_tensor(name, shape, dt))

        def sem(name):
            return ctx.enter_context(nc.semaphore(name))

        z_table = nc.dram_tensor("z_table", (NB * P, ZW), f32, kind="Internal").ap()
        xt_table = nc.dram_tensor("xt_table", (R * N, D), f32, kind="Internal").ap()

        iota_i = sb("iota_i", [P, NT], i32)
        pidx_i = sb("pidx_i", [P, 1], i32)
        iota = sb("iota", [P, P])
        iota16 = sb("iota16", [P, NT], f16)
        pidx = sb("pidx", [P, 1])
        pidx_c = sb("pidx_c", [P, NCH])
        ident = sb("ident", [P, P])
        ones16 = sb("ones16", [P, P], f16)
        zeros16 = sb("zeros16", [P, NT], f16)
        before_p = sb("before_p", [P, P], f16)
        upto_p = sb("upto_p", [P, P], f16)
        before_t = sb("before_t", [P, NCH, EC], f16)
        before_b = sb("before_b", [P, P], f16)

        xs = sb("xs", [P, NB, D])
        hn = sb("hn", [P, 2, D])
        hT = sb("hT", [P, 2, 2, P])
        zall = sb("zall", [P, NB, ZW])
        acc0 = sb("acc0", [P, NB, MW])
        acc1 = zall[:, :, 0:D]
        stats = sb("stats", [P, NB, 6])
        mean = sb("mean", [P, NB])
        var = sb("var", [P, NB])
        half = sb("half", [P, NB])
        rstd = sb("rstd", [P, NB])
        nmr = sb("nmr", [P, NB])
        epst = sb("epst", [P, 1])
        sdm = sb("sdm", [P, NB, 2 * H])
        top = sb("top", [P, H])
        top_all = sb("top_all", [P, H])
        tmp_m = sb("tmp_m", [P, NB, H])
        rden = sb("rden", [P, NB, H])
        w_rows = sb("w_rows", [P, 2, D])
        attn_cols = sb("attn_cols", [P, 2, 2 * H])
        w0T = sb("w0T", [P, 2, ZW])
        w1s = sb("w1s", [P, 2, R, D])
        bias_b = sb("bias_b", [P, D])

        e_src = sb("e_src", [EP, EC], i32)
        e_dst = sb("e_dst", [EP, EC], i32)
        e_typ = sb("e_typ", [EP, EC], i32)
        ti = sb("ti", [P, NT], i32)
        tj = sb("tj", [P, NT], i32)
        pos = sb("pos", [EP, EC])
        hi16 = sb("hi16", [EP, EC], f16)
        plo = sb("plo", [EP, EC])
        phi = sb("phi", [EP, EC])
        dig = sb("dig", [EP, 2, EC])
        scratch = sb("scratch", [P, NB * EC // 2])
        onehot_b = scratch[:, :].bitcast(f16).rearrange("p (b t) -> p b t", t=EC)
        stage = scratch[:, 0:2 * R * D].rearrange("p (s n) -> p s n", s=2)
        cntT = sb("cntT", [P, NCH, NB], f16)
        tiles_i = sb("tiles_i", [NB, 1], i32)
        tiles_f = sb("tiles_f", [NB, 1], f16)
        incl = sb("incl", [NB, 1])
        passed = sb("passed", [NB, NT], f16)
        Hs = sb("Hs", [EP, K, NT], f16)
        Ls = sb("Ls", [EP, K, 2, P], f16)
        srt = sb("srt", [P, 2, NT])
        idx = [sb(f"idx{w}", [P, NT], i32) for w in range(2)]
        lof = [sb(f"lof{w}", [P, NT + K]) for w in range(2)]
        bt = [sb(f"bt{w}", [P, NT + K], i32) for w in range(2)]

        G = sb("G", [P, 2 * K, ZW])
        O = sb("O", [P, 2 * K, P])
        OT = sb("OT", [P, K, P])
        msg = scratch[:, 0:K * MW].rearrange("p (k m) -> p k m", k=K)
        idx_now = sb("idx_now", [P, 2 * K], i32)
        ev = sb("ev", [P, K, H])
        ev2 = sb("ev2", [P, K, H])

        bank = [ctx.enter_context(nc.psum_tensor(f"bank{i}", [P, 512], f32)) for i in range(8)]

        s_x, s_xpad, s_edges, s_w0, s_attn, s_azero, s_w1, s_bias = (
            sem(n) for n in ("x_in", "x_pad", "edges_in", "w0_in", "attn_in", "attn_zeroed", "w1_in", "bias_in"))
        s_iota, s_const = sem("iota_made"), sem("consts_made")
        dve_own, act_own, pool_own = sem("dve_own"), sem("act_own"), sem("pool_own")
        s_oh, s_cnt, s_cntc, s_tot, s_tiles, s_incl, s_passed, s_bt, s_btc = (
            sem(n) for n in ("onehot_made", "counts_summed", "counts_copied", "totals_summed", "tiles_made",
                             "incl_summed", "passed_made", "bt_summed", "bt_copied"))
        s_rank, s_rankc = sem("rank_summed"), sem("rank_taken")
        s_hot, s_hotu, s_srt, s_srtc = sem("sort_onehots"), sem("sort_onehots_used"), sem("sorted"), sem("sorted_taken")
        s_sorted = sem("tiles_sorted")
        s_wt, s_wtc = sem("w0_turned"), sem("w0_turned_copied")
        s_var, s_std, s_ln = sem("var_ready"), sem("std_ready"), sem("ln_ready")
        s_h, s_hT, s_hTc, s_z, s_zc, s_zout = (
            sem(n) for n in ("h_ready", "h_turned", "h_turned_copied", "z_summed", "z_copied", "z_stored"))
        s_top, s_topa, s_sdm, s_acc0z = sem("top_ready"), sem("top_all_ready"), sem("sdm_ready"), sem("acc_zeroed")
        s_g = [sem(f"gathered{j}") for j in range(2 * K)]
        s_O, s_Ot, s_OTc, s_sd, s_ev, s_ex, s_msg, s_agg, s_acc = (
            sem(n) for n in ("onehot_n", "onehot_turned", "onehot_turned_copied", "scores_summed", "logits_ready",
                             "weights_ready", "msg_ready", "agg_summed", "agg_taken"))
        s_stage = sem("stage_free")
        s_xt, s_xta, s_xtd = sem("xt_summed"), sem("xt_copied_act"), sem("xt_copied_dve")
        s_xtout = [sem(f"xt_stored{u}") for u in range(2)]
        s_O1, s_agg1, s_acc1 = sem("onehot1"), sem("agg1_summed"), sem("agg1_taken")
        s_turn = sem("gather_turn")
        s_fin, s_out = sem("rows_final"), sem("out_stored")
        s_bn, s_x1, s_acc1z = sem("bn_stats_ready"), sem("x1_ready"), sem("acc1_zeroed")

        def row(t, b):
            return t[:, ds(b, 1), :].rearrange("p b d -> p (b d)")

        def buckets(eng, body):
            with eng.Fori(0, NB // 2) as i:
                for u in range(2):
                    body(i * 2 + u, u)
            body(NB - 1, 0)

        block = ctx.enter_context(nc.Block())
        full = (N // P) * P
        rest = N - full

        @block.sync
        def _(sp):
            sp.sem_inc(s_stage, 2)
            for tile, arr in ((e_src, src), (e_dst, dst), (e_typ, etype)):
                sp.dma_start(tile[:, :], arr.rearrange("(p t) -> p t", t=EC)).then_inc(s_edges, 16)
            sp.dma_start(xs[:, 0:NB - 1, :], x[0:full, :].rearrange("(b p) d -> p b d", p=P)).then_inc(s_x, 16)
            sp.wait_ge(s_xpad, 1)
            sp.dma_start(xs[0:rest, NB - 1, :], x[full:N, :]).then_inc(s_x, 16)
            sp.dma_start(w_rows[:, :, :], w0.rearrange("(j a) o d -> (a o) j d", a=2)).then_inc(s_w0, 16)
            sp.wait_ge(s_azero, 1)
            for j in range(2):
                for a in range(2):
                    for s in range(2):
                        c = s * H + 2 * j + a
                        sp.dma_start(attn_cols[a * DH:(a + 1) * DH, j, c:c + 1],
                                     attn[0:1, s * DH:(s + 1) * DH].rearrange("a d -> d a")).then_inc(s_attn, 16)
            for j in range(2):
                sp.dma_start(w1s[:, j, :, :], w1[:, j * P:(j + 1) * P, :].rearrange("r p o -> p r o")).then_inc(s_w1, 16)
            sp.dma_start(bias_b[:, :], bias.rearrange("(a d) -> a d", a=1).to_broadcast((P, D))).then_inc(s_bias, 16)

            def store_z(b, u):
                sp.wait_ge(s_zc, b + 3)
                sp.dma_start(z_table[ds(b * P, P), :], row(zall, b)).then_inc(s_zout, 16)
            buckets(sp, store_z)

            xt_v = xt_table.rearrange("(r n) d -> n r d", n=N)

            def store_xt(b, u, rows=P):
                sp.wait_ge(s_xta, 2 * b + 4)
                sp.wait_ge(s_xtd, 2 * b + 4)
                sp.dma_start(xt_v[ds(b * P, rows), :, :],
                             stage[0:rows, u, :].rearrange("p (r d) -> p r d", r=R)).then_inc(s_xtout[u], 16)
                sp.wait_ge(s_xtout[u], (b - u) * 8 + 16)
                sp.sem_inc(s_stage, 1)
            buckets(sp, lambda b, u: store_xt(b, u, rest if isinstance(b, int) else P))

            out_v = out[0:full, :].rearrange("(b p) d -> p b d", p=P)
            for c in range(NB // FC):
                sp.wait_ge(s_fin, c + 1)
                n = min(FC, NB - 1 - c * FC)
                sp.dma_start(out_v[:, c * FC:c * FC + n, :], xs[:, c * FC:c * FC + n, :]).then_inc(s_out, 16)
            sp.dma_start(out[full:N, :], xs[0:rest, NB - 1, :]).then_inc(s_out, 16)
            sp.wait_ge(s_out, 16 * (NB // FC + 1))

        @block.gpsimd
        def _(pool):
            pool.iota(iota_i[:, :], pattern=[[1, NT]], base=0, channel_multiplier=0).then_inc(s_iota, 1)
            pool.iota(pidx_i[:, :], pattern=[[0, 1]], base=0, channel_multiplier=1).then_inc(s_iota, 1)
            pool.wait_ge(s_top, 1)
            pool.partition_all_reduce(top_all[:, :], top[:, :], P, bass.bass_isa.ReduceOp.max).then_inc(s_topa, 1)

            def gather(table, w, row_len, free_sem, free_at):
                with pool.Fori(0, NBATCH // 2) as i:
                    for j in range(2 * K):
                        if j % K == 0:
                            s = j // K
                            pool.wait_ge(free_sem, free_at(i, s))
                            pool.sem_inc(s_turn, 1)
                            pool.tensor_copy(idx_now[:, j:j + K], idx[w][:, ds(i * 2 * K + j, K)]).then_inc(pool_own, 1)
                            pool.wait_ge(pool_own, i * 2 + (1 + s + w * NBATCH))
                            pool.sem_inc(s_turn, 1)
                        pool.indirect_dma_start(
                            G[:, j, 0:row_len], None, table,
                            bass.IndirectOffsetOnAxis(ap=idx_now[:, j:j + 1], axis=0),
                        ).then_inc(s_g[j], 16)

            pool.wait_ge(s_sorted, 1)
            pool.wait_ge(s_zout, 16 * NB)

            gather(z_table, 0, ZW, s_msg, lambda i, s: i * 4 + (2 * s + 2))

            pool.wait_ge(s_sorted, 2)
            pool.wait_ge(s_xtout[0], 16 * (NB // 2 + 1))
            pool.wait_ge(s_xtout[1], 16 * (NB // 2))
            pool.wait_ge(s_msg, 4 + 2 * NBATCH)
            gather(xt_table, 1, D, s_agg1, lambda i, s: (i * 2 + (s + 1)) * K)

        @block.vector
        def _(dve):
            own = Chain(dve, dve_own)
            V = nc.vector

            V.memset(xs[:, NB - 1, :], 0.0).then_inc(s_xpad, 1)
            V.memset(attn_cols[:, :, :], 0.0).then_inc(s_azero, 1)
            V.memset(epst[:, :], EPS)
            V.memset(ones16[:, :], 1.0)
            V.memset(zeros16[:, :], 0.0)
            for w in range(2):
                V.memset(lof[w][:, NT:NT + K], NO_NODE)
                V.memset(bt[w][:, NT:NT + K], 0)
            own(V.memset(acc0[:, :, :], 0.0))
            dve.wait_ge(s_iota, 2)
            V.tensor_copy(iota[:, :], iota_i[:, 0:P])
            V.tensor_copy(iota16[:, :], iota_i[:, :])
            own(V.tensor_copy(pidx[:, :], pidx_i[:, :]))
            for c in range(NCH):
                own(V.tensor_scalar(pidx_c[:, c:c + 1], pidx[:, :], float(c * CH), None, ALU.add))
            V.tensor_scalar(ident[:, :], iota[:, :], pidx[:, 0:1], None, ALU.is_equal)
            V.tensor_scalar(before_p[:, :], iota[:, :], pidx[:, 0:1], None, ALU.is_gt)
            V.tensor_scalar(upto_p[:, :], iota[:, :], pidx[:, 0:1], None, ALU.is_ge)
            V.tensor_scalar(before_b[:, :], iota[:, :], pidx[:, 0:1], float(P), ALU.is_gt, ALU.mult)
            for c in range(NCH):
                last = V.tensor_scalar(before_t[:, c, :], iota16[:, 0:EC], pidx_c[:, c:c + 1], None, ALU.is_gt)
            own(last)
            V.sem_inc(s_const, 1)
            V.sem_inc(s_hTc, 2)
            V.sem_inc(s_msg, 4)
            V.sem_inc(s_acc, 4)
            V.sem_inc(s_acc1, 8)
            V.sem_inc(s_xtd, 2)

            def norm_stats():
                m_e, m_o = stats[:, :, 1], stats[:, :, 4]
                v_e, v_o = stats[:, :, 2], stats[:, :, 5]

                def one(b, u):
                    V.bn_stats(row(stats, b), row(xs, b)).then_inc(s_bn, 1)
                buckets(dve, one)
                norm_stats.calls += 1
                dve.wait_ge(s_bn, NB * norm_stats.calls)
                V.tensor_tensor(mean[:, :], m_e, m_o, ALU.add)
                V.tensor_tensor(half[:, :], m_e, m_o, ALU.subtract)
                own(V.tensor_tensor(var[:, :], v_e, v_o, ALU.add))
                own(V.tensor_tensor(half[:, :], half[:, :], half[:, :], ALU.mult))
                V.tensor_scalar(mean[:, :], mean[:, :], 0.5, None, ALU.mult)
                own(V.tensor_scalar(var[:, :], var[:, :], 1.0 / D, None, ALU.mult))
                V.scalar_tensor_tensor(var[:, :], half[:, :], 0.25, var[:, :], ALU.mult, ALU.add).then_inc(s_var, 1)
                dve.wait_ge(s_std, norm_stats.calls)
                own(V.reciprocal(rstd[:, :], rstd[:, :]))
                V.scalar_tensor_tensor(nmr[:, :], mean[:, :], -1.0, rstd[:, :], ALU.mult, ALU.mult).then_inc(s_ln, 1)
            norm_stats.calls = 0

            def sort(w):
                key = e_dst if w == 0 else e_src
                a, b_ = ti[0:EP, 0:EC], tj[0:EP, 0:EC]
                if w == 0:
                    own(V.tensor_copy(a, e_src[:, :]))
                else:
                    own(V.tensor_scalar(a, e_typ[:, :], float(N), None, ALU.mult))
                    own(V.tensor_tensor(a, a, e_dst[:, :], ALU.add))
                own(V.tensor_scalar(b_, a, 4, None, ALU.logical_shift_right))
                V.tensor_copy(dig[:, 0, :], b_)
                own(V.tensor_scalar(a, a, 15, 7, ALU.bitwise_and, ALU.logical_shift_left))
                own(V.tensor_scalar(b_, key[:, :], P - 1, None, ALU.bitwise_and))
                own(V.tensor_tensor(a, a, b_, ALU.add))
                V.tensor_scalar(dig[:, 1, :], a, 1.0, None, ALU.add)
                own(V.tensor_scalar(b_, key[:, :], 7, None, ALU.logical_shift_right))
                own(V.tensor_copy(hi16[:, :], b_))
                if w:
                    dve.wait_ge(s_rank, NB)
                for b in range(NB):
                    last = V.tensor_scalar(onehot_b[0:EP, b, :], hi16[:, :], float(b), None, ALU.is_equal)
                last.then_inc(s_oh, 1)
                dve.wait_ge(s_cnt, w + 1)
                V.tensor_copy(cntT[0:CH, :, :], bank[0][0:CH, 0:NCH * NB].rearrange("p (c b) -> p c b", b=NB)
                              ).then_inc(s_cntc, 1)
                dve.wait_ge(s_tot, w + 1)
                own(V.tensor_scalar(tiles_i[:, :], bank[1][0:NB, 0:1], float(P - 1), None, ALU.add))
                own(V.tensor_scalar(tiles_i[:, :], tiles_i[:, :], 7, None, ALU.logical_shift_right))
                V.tensor_copy(tiles_f[:, :], tiles_i[:, :]).then_inc(s_tiles, 1)
                dve.wait_ge(s_incl, w + 1)
                own(V.tensor_copy(incl[:, :], bank[1][0:NB, 8:9]))
                V.tensor_scalar(passed[:, :], iota16[0:NB, :], incl[:, 0:1], None, ALU.is_ge).then_inc(s_passed, 1)
                for b in range(NB):
                    dve.wait_ge(s_rank, w * NB + b + 1)
                    if b:
                        dve.wait_ge(s_rankc, w * NB + b)
                    V.copy_predicated(pos[:, :], onehot_b[0:EP, b, :].bitcast(u16),
                                      bank[2 + b % 2][0:EP, 0:EC]).then_inc(s_rankc, 1)
                dve.wait_ge(s_bt, w + 1)
                V.tensor_scalar(bt[w][:, 0:NT], bank[0][:, 0:NT], float(NB - 1), None, ALU.min).then_inc(s_btc, 1)
                dve.wait_ge(s_rankc, (w + 1) * NB)
                own(V.tensor_copy(a, pos[:, :]))
                own(V.tensor_scalar(b_, a, P - 1, None, ALU.bitwise_and))
                V.tensor_copy(plo[:, :], b_)
                own(V.tensor_scalar(a, a, 7, None, ALU.logical_shift_right))
                own(V.tensor_copy(phi[:, :], a))
                with dve.Fori(0, EC // K) as i:
                    for k in range(K):
                        t = i * K + k
                        dve.wait_ge(s_hotu, t + (w * EC + 1))
                        V.tensor_scalar(Hs[:, k, :], iota16[0:EP, :], phi[:, ds(t, 1)], None, ALU.is_equal)
                        for g in range(2):
                            last = V.tensor_scalar(Ls[:, k, g, :], iota16[0:EP, 0:P], plo[:, ds(t, 1)],
                                                   dig[:, g, ds(t, 1)], ALU.is_equal, ALU.mult)
                        last.then_inc(s_hot, 1)
                dve.wait_ge(s_srt, w + 1)
                V.tensor_copy(srt[:, 0, :], bank[4][:, 0:NT])
                own(V.tensor_copy(srt[:, 1, :], bank[5][:, 0:NT]))
                V.sem_inc(s_srtc, 1)
                own(V.tensor_scalar(ti[:, :], srt[:, 1, :], -1.0, 0.0, ALU.add, ALU.max))
                V.tensor_scalar(srt[:, 1, :], srt[:, 1, :], 0.0, NO_NODE, ALU.is_equal, ALU.mult)
                own(V.tensor_scalar(tj[:, :], ti[:, :], P - 1, None, ALU.bitwise_and))
                V.tensor_tensor(lof[w][:, 0:NT], srt[:, 1, :], tj[:, :], ALU.add)
                own(V.tensor_scalar(ti[:, :], ti[:, :], 7, None, ALU.logical_shift_right))
                own(V.scalar_tensor_tensor(idx[w][:, :], srt[:, 0, :], 16.0, ti[:, :], ALU.mult, ALU.add))
                V.sem_inc(s_sorted, 1)

            dve.wait_ge(s_edges, 48)
            dve.wait_ge(s_x, 32)
            norm_stats()

            dve.wait_ge(s_wt, 1)
            own(V.tensor_copy(w0T[:, :, 0:D], bank[6][:, :].rearrange("p (j n) -> p j n", j=2)))
            V.tensor_copy(w0T[:, :, D:ZW], bank[7][:, 0:2 * 2 * H].rearrange("p (j n) -> p j n", j=2)).then_inc(s_wtc, 1)

            def copy_hT(base):
                def one(b, u):
                    dve.wait_ge(s_hT, b + (base + 1))
                    V.tensor_copy(hT[:, u, :, :].rearrange("p j n -> p (j n)"), bank[u][:, 0:D]).then_inc(s_hTc, 1)
                return one
            buckets(dve, copy_hT(2))

            dve.wait_ge(s_zc, NB + 2)
            V.tensor_copy(sdm[:, :, 0:H], zall[:, :, D + H:ZW])
            V.tensor_reduce(top[:, :], zall[:, :, D:D + H].rearrange("p b h -> p h b"), AX.X, ALU.max).then_inc(s_top, 1)
            dve.wait_ge(s_topa, 1)
            own(V.tensor_tensor(tmp_m[:, :, :], zall[:, :, D + H:ZW],
                                top_all[:, :].rearrange("p (a h) -> p a h", a=1).to_broadcast((P, NB, H)), ALU.add))
            own(V.scalar_tensor_tensor(sdm[:, :, H:2 * H], tmp_m[:, :, :], SLOPE, tmp_m[:, :, :], ALU.mult, ALU.max))
            V.sem_inc(s_sdm, 1)

            sort(0)
            sort(1)

            def onehots(w, t0, half_, done):
                for k in range(K):
                    last = V.tensor_scalar(O[:, half_ * K + k, :], iota[:, :], lof[w][:, ds(t0 + k, 1)], None, ALU.is_equal)
                last.then_inc(done, 1)

            onehots(0, 0, 0, s_O)
            n_link = own.n
            with dve.Fori(0, NBATCH // 2) as i:
                own.enter(i, 4)
                for s in range(2):
                    t0 = i * 2 * K + s * K
                    g = G[:, s * K:(s + 1) * K, :]
                    scores = bank[2][:, 0:K * 2 * H].rearrange("p (k c) -> p k c", k=K)
                    dve.wait_ge(s_sd, i * 2 + (s + 1))
                    for j in range(K):
                        dve.wait_ge(s_g[s * K + j], i * 16 + 16)
                    own(V.tensor_tensor(ev[:, :, :], g[:, :, D:D + H], scores[:, :, 0:H], ALU.add))
                    own(V.scalar_tensor_tensor(ev2[:, :, :], ev[:, :, :], SLOPE, ev[:, :, :], ALU.mult, ALU.max))
                    V.tensor_tensor(ev[:, :, :], ev2[:, :, :], scores[:, :, H:2 * H], ALU.subtract).then_inc(s_ev, 1)
                    onehots(0, t0 + K, 1 - s, s_O)
                    dve.wait_ge(s_ex, i * 2 + (s + 1))
                    for q in range(2):
                        ks = slice(q * K // 2, (q + 1) * K // 2)
                        V.tensor_tensor(msg[:, ks, 0:D].rearrange("p k (h d) -> p k h d", h=H),
                                        g[:, ks, 0:D].rearrange("p k (h d) -> p k h d", h=H),
                                        msg[:, ks, D:MW].rearrange("p k (h a) -> p k h a", a=1).to_broadcast((P, K // 2, H, DH)),
                                        ALU.mult).then_inc(s_msg, 1)
                    for k in range(K):
                        b = V.value_load(bt[0][0:1, ds(t0 + k, 1)], min_val=0, max_val=NB - 1)
                        dve.wait_ge(s_agg, t0 + (k + 1))
                        dve.wait_ge(s_acc, t0 + (k + 4))
                        V.tensor_tensor(row(acc0, b), row(acc0, b), bank[4 + k % 4][:, 0:MW], ALU.add).then_inc(s_acc, 1)
                own.leave(4, NBATCH // 2)

            dve.wait_ge(s_acc, NT + 4)
            own(V.tensor_scalar(rden[:, :, :], acc0[:, :, D:MW], 1e-9, None, ALU.max))
            own(V.reciprocal(rden[:, :, :], rden[:, :, :]))

            with dve.Fori(0, NB) as b:
                own.enter(b, 1)
                q = row(acc0, b)[:, 0:D].rearrange("p (h d) -> p h d", h=H)
                own(V.tensor_tensor(q, q, row(rden, b).rearrange("p (h a) -> p h a", a=1).to_broadcast((P, H, DH)), ALU.mult))
                V.tensor_tensor(row(xs, b), row(xs, b), row(acc0, b)[:, 0:D], ALU.add).then_inc(s_x1, 1)
                own.leave(1, NB)
            dve.wait_ge(s_x1, NB)
            norm_stats()
            V.memset(acc1, 0.0).then_inc(s_acc1z, 1)

            def xt_dve(b, u):
                copy_hT(2 + NB)(b, u)
                dve.wait_ge(s_stage, b + 1)
                for c in range(2):
                    dve.wait_ge(s_xt, b * 4 + (c + 3))
                    V.tensor_copy(stage[:, u, (c + 2) * 512:(c + 3) * 512], bank[6 + c][:, :]).then_inc(s_xtd, 1)
            buckets(dve, xt_dve)

            dve.wait_ge(s_acc1z, 1)
            onehots(1, 0, 0, s_O1)
            with dve.Fori(0, NBATCH // 2) as i:
                for s in range(2):
                    t0 = i * 2 * K + s * K
                    onehots(1, t0 + K, 1 - s, s_O1)
                    for k in range(K):
                        b = V.value_load(bt[1][0:1, ds(t0 + k, 1)], min_val=0, max_val=NB - 1)
                        dve.wait_ge(s_agg1, t0 + (k + 1 + 2 * K))
                        dve.wait_ge(s_acc1, t0 + (k + 8))
                        r = acc1[:, ds(b, 1), :].rearrange("p b d -> p (b d)")
                        V.tensor_tensor(r, r, bank[k][:, 0:D], ALU.add).then_inc(s_acc1, 1)

            dve.wait_ge(s_acc1, NT + 8)
            dve.wait_ge(s_bias, 16)
            with dve.Fori(0, NB // FC) as c:
                own.enter(c, 2)
                r = acc1[:, ds(c * FC, FC), :]
                own(V.tensor_tensor(r, r, bias_b[:, :].rearrange("p (a d) -> p a d", a=1).to_broadcast((P, FC, D)), ALU.add))
                own(V.tensor_scalar(r, r, 0.0, None, ALU.max))
                q = xs[:, ds(c * FC, FC), :]
                V.tensor_tensor(q, q, r, ALU.add).then_inc(s_fin, 1)
                own.leave(2, NB // FC)

        @block.scalar
        def _(act):
            A = nc.scalar
            A.sem_inc(s_xta, 2)
            A.sem_inc(s_zc, 2)

            def norm(w):
                act.wait_ge(s_var, w + 1)
                A.activation(rstd[:, :], var[:, :], ACT.Sqrt, bias=epst[:, 0:1]).then_inc(s_std, 1)
                act.wait_ge(s_ln, w + 1)

            def make_h(base):
                def one(b, u):
                    act.wait_ge(s_hT, b + (base + 1))
                    A.activation(hn[:, u, :], row(xs, b), ACT.Relu, bias=nmr[:, ds(b, 1)], scale=rstd[:, ds(b, 1)]
                                 ).then_inc(s_h, 1)
                return one

            act.wait_ge(s_const, 1)
            norm(0)
            def layer0_table(b, u):
                make_h(0)(b, u)
                act.wait_ge(s_z, b + 1)
                A.copy(row(zall, b), bank[2 + u][:, 0:ZW]).then_inc(s_zc, 1)
            buckets(act, layer0_table)

            def turned(base):
                for q in range(2):
                    act.wait_ge(s_Ot, base + (q + 1))
                    A.copy(OT[:, q * K // 2:(q + 1) * K // 2, :].rearrange("p k e -> p (k e)"), bank[q][:, :]).then_inc(s_OTc, 1)
            turned(0)
            with act.Fori(0, NBATCH // 2) as i:
                for s in range(2):
                    act.wait_ge(s_ev, i * 2 + (s + 1))
                    A.activation(msg[:, :, D:MW], ev[:, :, :], ACT.Exp).then_inc(s_ex, 1)
                    turned(i * 4 + (2 * s + 2))

            norm(1)
            def layer1_table(b, u):
                make_h(NB)(b, u)
                act.wait_ge(s_stage, b + 1)
                for c in range(2):
                    act.wait_ge(s_xt, b * 4 + (c + 1))
                    A.copy(stage[:, u, c * 512:(c + 1) * 512], bank[4 + c][:, :]).then_inc(s_xta, 1)
            buckets(act, layer1_table)

        @block.tensor
        def _(pe):
            T = nc.tensor
            T.sem_inc(s_hT, 2)
            T.sem_inc(s_hotu, K)
            T.sem_inc(s_agg1, 2 * K)
            pe.wait_ge(s_const, 1)
            pe.wait_ge(s_w0, 16)
            pe.wait_ge(s_attn, 16 * 8)
            for k in range(2):
                for j in range(2):
                    T.transpose(bank[6][:, (k * 2 + j) * P:(k * 2 + j + 1) * P], w_rows[:, j, k * P:(k + 1) * P], ident[:, :])
            for k in range(2):
                for j in range(2):
                    last = T.matmul(bank[7][:, k * 2 * H:(k + 1) * 2 * H], w_rows[:, j, k * P:(k + 1) * P],
                                    attn_cols[:, j, :], start=(j == 0), stop=(j == 1))
            last.then_inc(s_wt, 1)

            def turn_h(b, u, base):
                pe.wait_ge(s_h, b + (base + 1))
                pe.wait_ge(s_hTc, b + (base + 1))
                for j in range(2):
                    last = T.transpose(bank[u][:, j * P:(j + 1) * P], hn[:, u, j * P:(j + 1) * P], ident[:, :])
                last.then_inc(s_hT, 1)
                pe.wait_ge(s_hTc, b + (base + 3))

            pe.wait_ge(s_wtc, 1)
            def layer0_table(b, u):
                turn_h(b, u, 0)
                pe.wait_ge(s_zc, b + 1)
                for j in range(2):
                    last = T.matmul(bank[2 + u][:, 0:ZW], hT[:, u, j, :], w0T[:, j, :], start=(j == 0), stop=(j == 1))
                last.then_inc(s_z, 1)
            buckets(pe, layer0_table)

            def sort(w):
                pe.wait_ge(s_oh, w + 1)
                for c in range(NCH):
                    for b in range(NB):
                        last = T.matmul(bank[0][0:CH, c * NB + b:c * NB + b + 1], onehot_b[0:EP, b, c * CH:(c + 1) * CH],
                                        ones16[0:EP, 0:1], start=True, stop=True)
                last.then_inc(s_cnt, 1)
                pe.wait_ge(s_cntc, w + 1)
                for c in range(NCH):
                    last = T.matmul(bank[1][0:NB, 0:1], cntT[0:CH, c, :], ones16[0:CH, 0:1], start=(c == 0), stop=(c == NCH - 1))
                last.then_inc(s_tot, 1)
                pe.wait_ge(s_tiles, w + 1)
                T.matmul(bank[1][0:NB, 8:9], upto_p[0:NB, 0:NB], tiles_f[:, :], start=True, stop=True).then_inc(s_incl, 1)
                for b in range(NB):
                    if w * NB + b >= 2:
                        pe.wait_ge(s_rankc, w * NB + b - 1)
                    o = bank[2 + b % 2][0:EP, 0:EC]
                    T.matmul(o, before_p[0:EP, 0:EP], onehot_b[0:EP, b, :], start=True, stop=False)
                    for c in range(NCH):
                        T.matmul(o, cntT[0:CH, c, b:b + 1].to_broadcast((CH, EP)), before_t[0:CH, c, :], start=False, stop=False)
                    T.matmul(o, tiles_f[:, 0:1].to_broadcast((NB, EP)), before_b[0:NB, b:b + 1].to_broadcast((NB, EC)),
                             start=False, stop=True).then_inc(s_rank, 1)
                pe.wait_ge(s_passed, w + 1)
                T.matmul(bank[0][:, 0:NT], ones16[0:NB, :], passed[:, :], start=True, stop=True).then_inc(s_bt, 1)
                if w:
                    pe.wait_ge(s_srtc, w)
                for g in range(2):
                    T.matmul(bank[4 + g][:, 0:NT], zeros16[0:EP, 0:P], zeros16[0:EP, :], start=True, stop=False)
                with pe.Fori(0, EC // K) as i:
                    for k in range(K):
                        pe.wait_ge(s_hot, i * K + (k + 1 + w * EC))
                        for g in range(2):
                            last = T.matmul(bank[4 + g][:, 0:NT], Ls[:, k, g, :], Hs[:, k, :], start=False, stop=False)
                        last.then_inc(s_hotu, 1)
                for g in range(2):
                    last = T.matmul(bank[4 + g][:, 0:NT], zeros16[0:EP, 0:P], zeros16[0:EP, :], start=False, stop=True)
                last.then_inc(s_srt, 1)
            sort(0)
            sort(1)

            def turn_onehots(half_, batch):
                pe.wait_ge(s_O, batch + 1)
                for q in range(2):
                    for k in range(q * K // 2, (q + 1) * K // 2):
                        last = T.transpose(bank[q][:, (k % 4) * P:(k % 4 + 1) * P], O[:, half_ * K + k, :], ident[:, :])
                    last.then_inc(s_Ot, 1)

            def scores(batch, t0):
                pe.wait_ge(s_OTc, batch * 2 + 2)
                for k in range(K):
                    b = T.value_load(bt[0][0:1, ds(t0 + k, 1)], min_val=0, max_val=NB - 1)
                    last = T.matmul(bank[2][:, k * 2 * H:(k + 1) * 2 * H], OT[:, k, :], row(sdm, b), start=True, stop=True)
                last.then_inc(s_sd, 1)

            pe.wait_ge(s_btc, 1)
            pe.wait_ge(s_sdm, 1)
            turn_onehots(0, 0)
            scores(0, 0)
            with pe.Fori(0, NBATCH // 2) as i:
                for s in range(2):
                    t0 = i * 2 * K + s * K
                    turn_onehots(1 - s, i * 2 + (s + 1))
                    for k in range(K):
                        if k % 4 == 0:
                            pe.wait_ge(s_msg, i * 4 + (2 * s + k // 4 + 5))
                        if k == K // 2:
                            pe.wait_ge(s_ev, i * 2 + (s + 1))
                            scores(i * 2 + (s + 1), t0 + K)
                        pe.wait_ge(s_acc, t0 + (k + 1))
                        T.matmul(bank[4 + k % 4][:, 0:MW], O[:, s * K + k, :], msg[:, k, :], start=True, stop=True).then_inc(s_agg, 1)

            pe.wait_ge(s_w1, 32)
            def layer1_table(b, u):
                turn_h(b, u, NB)
                for c in range(4):
                    pe.wait_ge(s_xta if c < 2 else s_xtd, b * 2 + (c % 2 + 1))
                    for q in range(2):
                        for j in range(2):
                            last = T.matmul(bank[4 + c][:, q * D:(q + 1) * D], hT[:, u, j, :], w1s[:, j, 2 * c + q, :],
                                            start=(j == 0), stop=(j == 1))
                    last.then_inc(s_xt, 1)
            buckets(pe, layer1_table)

            with pe.Fori(0, NBATCH // 2) as i:
                for s in range(2):
                    t0 = i * 2 * K + s * K
                    pe.wait_ge(s_O1, i * 2 + (s + 1))
                    for k in range(K):
                        pe.wait_ge(s_g[s * K + k], i * 16 + 16 * (NBATCH // 2 + 1))
                        pe.wait_ge(s_acc1, t0 + (k + 1))
                        T.matmul(bank[k][:, 0:D], O[:, s * K + k, :], G[:, s * K + k, 0:D], start=True, stop=True).then_inc(s_agg1, 1)


_INS = ['x', 'src', 'dst', 'edge_type_8', 'L0_gnn_W', 'L0_gnn_attn', 'L1_gnn_weight', 'L1_gnn_bias']
_OUTS = [((N, D), 'float32')]


def kernel(**inputs):
    import numpy as _np
    import concourse.bacc as _bacc
    from concourse import mybir as _mybir
    from concourse.bass_utils import run_bass_kernel_spmd as _run

    nc = _bacc.Bacc("TRN2", target_bir_lowering=False, num_devices=1)
    arrays, args = {}, []
    for name in _INS:
        a = _np.ascontiguousarray(inputs[name])
        arrays[f"in_{name}_dram"] = a
        args.append(nc.dram_tensor(f"in_{name}_dram", a.shape, _mybir.dt.from_np(a.dtype), kind="ExternalInput").ap())
    for i, (shape, dtype) in enumerate(_OUTS):
        dt = _mybir.dt.from_np(_np.dtype(dtype))
        args.append(nc.dram_tensor(f"out_{i}_dram", shape, dt, kind="ExternalOutput").ap())
    build(nc, *args)
    r = _run(nc, [arrays], core_ids=[0])
    return r.results[0]["out_0_dram"]
```

```python
import concourse.bass as bass
from concourse import mybir
from contextlib import ExitStack

P = 128
N, E, D = 3125, 50000, 256
H, DH, R = 4, 64, 8
NB = -(-N // P)
EP, EC = 125, 400
NT = EC // 8 * 8 + 16
CH, NCH = 100, 4
ZW = D + 2 * H
MW = D + H
K = 8
NBATCH = NT // K
FC = 5
C0, C1 = 4, 8
EPS = 1e-5
SLOPE = 0.01
NO_NODE = -200.0

assert EP * EC == E and CH * NCH == EC and E // P + NB <= NT and NB % FC == 0 and NB % 2 == 1 and NBATCH % 2 == 0


assert C0 * NBATCH + C1 * (NB - 1) == EC and C0 * 2 == C1 == K
TG = NT // NCH


class Chain:

    def __init__(self, eng, sem):
        self.eng, self.sem, self.n, self.off = eng, sem, 0, 0

    def __call__(self, ins):
        ins.then_inc(self.sem, 1)
        self.n += 1
        self.eng.wait_ge(self.sem, self.off + self.n)

    def enter(self, i, per):
        self.off = i * per
        self.start = self.n

    def leave(self, per, trips):
        assert self.n - self.start == per, (self.n - self.start, per)
        self.off = 0
        self.n = self.start + per * trips


def build(nc, x, src, dst, etype, w0, attn, w1, bias, out):
    f32, f16, bf16, i32, u16 = (mybir.dt.float32, mybir.dt.float16, mybir.dt.bfloat16, mybir.dt.int32,
                                mybir.dt.uint16)
    ALU, ACT, AX = mybir.AluOpType, mybir.ActivationFunctionType, mybir.AxisListType
    ds = bass.ds

    with ExitStack() as ctx:
        def sb(name, shape, dt=f32):
            return ctx.enter_context(nc.sbuf_tensor(name, shape, dt))

        def sem(name):
            return ctx.enter_context(nc.semaphore(name))

        z_table = nc.dram_tensor("z_table", (NB * P, ZW), f32, kind="Internal").ap()
        xt_table = nc.dram_tensor("xt_table", (R * N, D), f32, kind="Internal").ap()

        key_pad = nc.dram_tensor("key_pad", (E + P,), i32, kind="Internal").ap()
        row_pad = nc.dram_tensor("row_pad", (E + P,), i32, kind="Internal").ap()

        iota_i = sb("iota_i", [P, NT], i32)
        pidx_i = sb("pidx_i", [P, 1], i32)
        iota = sb("iota", [P, P])
        iota16 = sb("iota16", [P, NT], f16)
        pidx = sb("pidx", [P, 1])
        pidx_c = sb("pidx_c", [P, NCH])
        ident = sb("ident", [P, P])
        ones16 = sb("ones16", [P, P], f16)
        zeros16 = sb("zeros16", [P, NT + 1], f16)
        ident16 = sb("ident16", [P, P], bf16)
        ones_f = sb("ones_f", [EP, P])
        step16 = sb("step16", [P, NT + 1], f16)
        tile_e = sb("tile_e", [TG, NCH])
        tile_e_i = sb("tile_e_i", [TG, NCH], i32)
        pads = sb("pads", [1, 2, P], i32)
        before_p = sb("before_p", [P, P], f16)
        upto_p = sb("upto_p", [P, P], f16)
        before_t = sb("before_t", [P, NCH, EC], f16)
        before_b = sb("before_b", [P, P], f16)

        G = sb("G", [P, 2 * K, ZW])
        G_flat = G[:, :, :].rearrange("p k z -> p (k z)")
        w1s = G_flat[:, 0:2 * R * D].rearrange("p (j r o) -> p j r o", j=2, r=R)

        xs = sb("xs", [P, NB, D])
        hn = sb("hn", [P, 2, D])
        hT = sb("hT", [P, 2, 2, P])
        zall = sb("zall", [P, NB, ZW])
        acc0 = sb("acc0", [P, NB, MW])
        acc1 = zall[:, :, 0:D]
        stats = sb("stats", [P, NB, 6])
        mean = sb("mean", [P, NB])
        var = sb("var", [P, NB])
        half = sb("half", [P, NB])
        rstd = sb("rstd", [P, NB])
        nmr = sb("nmr", [P, NB])
        epst = sb("epst", [P, 1])
        sdm = sb("sdm", [P, NB, 2 * H])
        top = sb("top", [P, H])
        top_all = sb("top_all", [P, H])
        tmp_m = sb("tmp_m", [P, NB, H])
        rden = sb("rden", [P, NB, H])
        w_rows = sb("w_rows", [P, 2, D])
        attn_cols = sb("attn_cols", [P, 2, 2 * H])
        w0T = sb("w0T", [P, 2, ZW])
        bias_b = sb("bias_b", [P, D])

        e_src = sb("e_src", [EP, EC], i32)
        e_dst = sb("e_dst", [EP, EC], i32)
        e_typ = sb("e_typ", [EP, EC], i32)
        Hs = sb("Hs", [EP, K, NT + 2], f16)
        Ls = sb("Ls", [EP, K, 2, P], f16)
        Hs_i = Hs[:, :, :].rearrange("p k t -> p (k t)").bitcast(i32)
        e_nxt = Ls[:, :, :, :].rearrange("p k g n -> p (k g n)").bitcast(i32)[:, 0:EC]
        ti = sb("ti", [P, NT], i32)
        tj = sb("tj", [P, NT], i32)
        pos = sb("pos", [EP, EC])
        hi16 = sb("hi16", [EP, EC], f16)
        hn16 = sb("hn16", [EP, EC], f16)
        drops = sb("drops", [EP, 1])
        sort_it = sb("sort_it", [P, 1], i32)
        plo = [G_flat[0:EP, 0:EC], sb("plo1", [EP, EC])]
        nphi = [G_flat[0:EP, EC:2 * EC], sb("nphi1", [EP, EC])]
        dig = [G_flat[0:EP, 2 * EC:4 * EC].rearrange("p (g t) -> p g t", g=2), sb("dig1", [EP, 2, EC])]
        scratch = sb("scratch", [P, NB * EC // 2])
        onehot_b = scratch[:, :].bitcast(f16).rearrange("p (b t) -> p b t", t=EC)
        stage = scratch[:, 0:2 * R * D].rearrange("p (s n) -> p s n", s=2)
        cntT = sb("cntT", [P, NCH, NB], f16)
        tiles_i = sb("tiles_i", [NB, 1], i32)
        tiles_f = sb("tiles_f", [NB, 1], f16)
        tiles_s = sb("tiles_s", [NB, 1])
        short = sb("short", [NB, 1], f16)
        incl = sb("incl", [NB, 1])
        passed = sb("passed", [NB, NT], f16)
        first_e = sb("first_e", [TG, NCH])
        first_i = sb("first_i", [TG, NCH], i32)
        tile_b = sb("tile_b", [TG, NCH])
        keyT, rowT = (Hs_i[0:TG, n * NCH * P:(n + 1) * NCH * P].rearrange("p (c e) -> p c e", c=NCH) for n in range(2))
        keyF = keyT[:, :, :].bitcast(f32)
        rowF = rowT[:, :, :].bitcast(f32)
        srt = sb("srt", [P, 2, NT + 1])
        idx = [sb(f"idx{w}", [P, NT], i32) for w in range(2)]
        lof = [sb(f"lof{w}", [P, NT + K]) for w in range(2)]
        bt = [sb(f"bt{w}", [P, NT + K], i32) for w in range(2)]

        O = sb("O", [P, 2 * K, P])
        Ob = sb("Ob", [P, K, P], bf16)
        OT = sb("OT", [P, K, P])
        msg = scratch[:, 0:K * MW].rearrange("p (k m) -> p k m", k=K)
        idx_now = sb("idx_now", [P, 2 * K], i32)
        ev = sb("ev", [P, K, H])
        ev2 = sb("ev2", [P, K, H])

        bank = [ctx.enter_context(nc.psum_tensor(f"bank{i}", [P, 512], f32)) for i in range(8)]

        s_x, s_xpad, s_edges, s_w0, s_attn, s_azero, s_w1, s_bias = (
            sem(n) for n in ("x_in", "x_pad", "edges_in", "w0_in", "attn_in", "attn_zeroed", "w1_in", "bias_in"))
        s_iota, s_const = sem("iota_made"), sem("consts_made")
        dve_own, act_own, pool_own = sem("dve_own"), sem("act_own"), sem("pool_own")
        def per_sort(name):
            return [sem(f"{name}{w}") for w in range(2)]
        s_oh, s_cnt, s_cntc, s_tot, s_tiles, s_incl, s_passed, s_bt, s_btc = (
            per_sort(n) for n in ("onehots_made", "counts_summed", "counts_copied", "totals_summed", "tiles_made",
                                  "incl_summed", "passed_made", "bt_summed", "bt_copied"))
        s_rank, s_rankc, s_L, s_H, s_hotu, s_srt, s_sorted = (
            per_sort(n) for n in ("rank_summed", "rank_taken", "place_onehots", "tile_steps", "columns_sorted",
                                  "sort_summed", "tiles_sorted"))
        s_key, s_keyn, s_padk = sem("keys_padded"), sem("next_keys_in"), sem("pad_made")
        s_drop, s_dropc, s_flag = sem("drops_counted"), sem("drops_summed"), sem("sort_flag")
        s_first, s_firstc, s_slices, s_tl, s_tt = (
            sem(n) for n in ("first_summed", "first_made", "slices_in", "slices_local", "slices_turned"))
        s_sorting = sem("places_made")
        slow_own = sem("dve_own_in_sort")
        s_wt, s_wtc = sem("w0_turned"), sem("w0_turned_copied")
        s_var, s_std, s_ln = sem("var_ready"), sem("std_ready"), sem("ln_ready")
        s_h, s_hT, s_hTc, s_z, s_zc, s_zout = (
            sem(n) for n in ("h_ready", "h_turned", "h_turned_copied", "z_summed", "z_copied", "z_stored"))
        s_top, s_topa, s_sdm, s_acc0z = sem("top_ready"), sem("top_all_ready"), sem("sdm_ready"), sem("acc_zeroed")
        s_g = [sem(f"gathered{j}") for j in range(2 * K)]
        s_O32 = sem("onehot_f32")
        s_O, s_Ot, s_OTc, s_sd, s_ev, s_ex, s_msg, s_agg, s_acc = (
            sem(n) for n in ("onehot_n", "onehot_turned", "onehot_turned_copied", "scores_summed", "logits_ready",
                             "weights_ready", "msg_ready", "agg_summed", "agg_taken"))
        s_stage = sem("stage_free")
        s_xt, s_xta, s_xtd = sem("xt_summed"), sem("xt_copied_act"), sem("xt_copied_dve")
        s_xtout = [sem(f"xt_stored{u}") for u in range(2)]
        s_O1, s_agg1, s_acc1 = sem("onehot1"), sem("agg1_summed"), sem("agg1_taken")
        s_turn = sem("gather_turn")
        s_fin, s_out = sem("rows_final"), sem("out_stored")
        s_bn, s_x1, s_acc1z = sem("bn_stats_ready"), sem("x1_ready"), sem("acc1_zeroed")

        def row(t, b):
            return t[:, ds(b, 1), :].rearrange("p b d -> p (b d)")

        def buckets(eng, *steps):
            with eng.Fori(0, NB // 2) as i:
                for step in steps:
                    for u in range(2):
                        step(i * 2 + u, u, i)
            for step in steps:
                step(NB - 1, 0, NB // 2)

        block = ctx.enter_context(nc.Block())
        full = (N // P) * P
        rest = N - full

        @block.sync
        def _(sp):
            sp.sem_inc(s_stage, 2)
            def columns(a):
                return a.rearrange("(p t) -> p t", t=EC)
            for tile, arr in ((e_src, src), (e_typ, etype), (e_dst, dst)):
                sp.dma_start(tile[:, :], columns(arr)).then_inc(s_edges, 16)
            sp.wait_ge(s_padk, 1)
            for a, (pad, arr) in enumerate(((key_pad, dst), (row_pad, src))):
                sp.dma_start(columns(pad[0:E]), columns(arr)).then_inc(s_key, 16)
                sp.dma_start(pad[E:E + P].rearrange("(a p) -> a p", a=1), pads[:, a, :]).then_inc(s_key, 16)
            sp.dma_start(xs[:, 0:NB - 1, :], x[0:full, :].rearrange("(b p) d -> p b d", p=P)).then_inc(s_x, 16)
            sp.wait_ge(s_key, 64)
            sp.dma_start(e_nxt[:, :], columns(key_pad[1:E + 1])).then_inc(s_keyn, 16)
            sp.wait_ge(s_xpad, 1)
            sp.dma_start(xs[0:rest, NB - 1, :], x[full:N, :]).then_inc(s_x, 16)
            sp.dma_start(w_rows[:, :, :], w0.rearrange("(j a) o d -> (a o) j d", a=2)).then_inc(s_w0, 16)
            sp.wait_ge(s_azero, 1)
            for j in range(2):
                for a in range(2):
                    for s in range(2):
                        c = s * H + 2 * j + a
                        sp.dma_start(attn_cols[a * DH:(a + 1) * DH, j, c:c + 1],
                                     attn[0:1, s * DH:(s + 1) * DH].rearrange("a d -> d a")).then_inc(s_attn, 16)
            sp.dma_start(bias_b[:, :], bias.rearrange("(a d) -> a d", a=1).to_broadcast((P, D))).then_inc(s_bias, 16)

            def store_z(b, u, i):
                sp.wait_ge(s_zc, b + 3)
                sp.dma_start(z_table[ds(b * P, P), :], row(zall, b)).then_inc(s_zout, 16)
            buckets(sp, store_z)

            sp.wait_ge(s_msg, 4 + 2 * NBATCH)
            for j in range(2):
                sp.dma_start(w1s[:, j, :, :], w1[:, j * P:(j + 1) * P, :].rearrange("r p o -> p r o")).then_inc(s_w1, 16)

            xt_v = xt_table.rearrange("(r n) d -> n r d", n=N)

            def store_xt(b, u, i):
                rows = rest if isinstance(b, int) else P
                sp.wait_ge(s_xta, 2 * b + 4)
                sp.wait_ge(s_xtd, 2 * b + 4)
                sp.dma_start(xt_v[ds(b * P, rows), :, :],
                             stage[0:rows, u, :].rearrange("p (r d) -> p r d", r=R)).then_inc(s_xtout[u], 16)
                sp.wait_ge(s_xtout[u], i * 16 + 16)
                sp.sem_inc(s_stage, 1)
            buckets(sp, store_xt)

            out_v = out[0:full, :].rearrange("(b p) d -> p b d", p=P)
            for c in range(NB // FC):
                sp.wait_ge(s_fin, c + 1)
                n = min(FC, NB - 1 - c * FC)
                sp.dma_start(out_v[:, c * FC:c * FC + n, :], xs[:, c * FC:c * FC + n, :]).then_inc(s_out, 16)
            sp.dma_start(out[full:N, :], xs[0:rest, NB - 1, :]).then_inc(s_out, 16)
            sp.wait_ge(s_out, 16 * (NB // FC + 1))

        @block.gpsimd
        def _(pool):
            pool.iota(iota_i[:, :], pattern=[[1, NT]], base=0, channel_multiplier=0).then_inc(s_iota, 1)
            pool.iota(pidx_i[:, :], pattern=[[0, 1]], base=0, channel_multiplier=1).then_inc(s_iota, 1)
            pool.iota(tile_e_i[:, :], pattern=[[TG * P, NCH]], base=0, channel_multiplier=P).then_inc(s_iota, 1)
            pool.memset(acc0[:, :, :], 0.0).then_inc(s_acc0z, 1)
            pool.wait_ge(s_top, 1)
            pool.partition_all_reduce(top_all[:, :], top[:, :], P, bass.bass_isa.ReduceOp.max).then_inc(s_topa, 1)

            def gather(table, w, row_len, free_sem, free_at):
                with pool.Fori(0, NBATCH // 2) as i:
                    for j in range(2 * K):
                        if j % K == 0:
                            s = j // K
                            pool.wait_ge(free_sem, free_at(i, s))
                            pool.sem_inc(s_turn, 1)
                            pool.tensor_copy(idx_now[:, j:j + K], idx[w][:, ds(i * 2 * K + j, K)]).then_inc(pool_own, 1)
                            pool.wait_ge(pool_own, i * 2 + (1 + s + w * NBATCH))
                            pool.sem_inc(s_turn, 1)
                        pool.indirect_dma_start(
                            G[:, j, 0:row_len], None, table,
                            bass.IndirectOffsetOnAxis(ap=idx_now[:, j:j + 1], axis=0),
                        ).then_inc(s_g[j], 16)

            pool.wait_ge(s_flag, 1)
            pool.wait_ge(s_key, 64)
            pool.wait_ge(s_firstc, 1)
            with pool.If(pool.value_load(sort_it[0:1, 0:1], min_val=0, max_val=1) < 1):
                for c in range(NCH):
                    for pad, tile in ((key_pad, keyT), (row_pad, rowT)):
                        pool.indirect_dma_start(tile[:, c, :], None, pad.rearrange("(n a) -> n a", a=1),
                                                bass.IndirectOffsetOnAxis(ap=first_i[:, c:c + 1], axis=0)
                                                ).then_inc(s_slices, 16)

            pool.wait_ge(s_sorted[0], 1)
            pool.wait_ge(s_zout, 16 * NB)

            gather(z_table, 0, ZW, s_msg, lambda i, s: i * 4 + (2 * s + 2))

            pool.wait_ge(s_sorted[1], 1)
            pool.wait_ge(s_xtout[0], 16 * (NB // 2 + 1))
            pool.wait_ge(s_xtout[1], 16 * (NB // 2))
            pool.wait_ge(s_msg, 4 + 2 * NBATCH)
            gather(xt_table, 1, D, s_agg1, lambda i, s: (i * 2 + (s + 1)) * K)

        def load_buckets(eng, name, w, t0):
            regs = [eng.alloc_register(f"bucket_{name}_{k}") for k in range(K)]
            eng.load(regs, bt[w][0:1, ds(t0, K)])
            return [eng.snap(r, donate=True, min_val=0, max_val=NB - 1) for r in regs]

        @block.vector
        def _(dve):
            own = Chain(dve, dve_own)
            V = nc.vector

            V.memset(pads[:, 0, :], NB * P)
            V.memset(pads[:, 1, :], 0).then_inc(s_padk, 1)
            V.memset(xs[:, NB - 1, :], 0.0).then_inc(s_xpad, 1)
            V.memset(attn_cols[:, :, :], 0.0).then_inc(s_azero, 1)
            V.memset(epst[:, :], EPS)
            V.memset(ones16[:, :], 1.0)
            V.memset(ones_f[:, :], 1.0)
            V.memset(zeros16[:, :], 0.0)
            for w in range(2):
                V.memset(lof[w][:, NT:NT + K], NO_NODE)
                own(V.memset(bt[w][:, NT:NT + K], 0))
            dve.wait_ge(s_iota, 3)
            V.tensor_copy(iota[:, :], iota_i[:, 0:P])
            V.tensor_copy(iota16[:, :], iota_i[:, :])
            V.tensor_copy(tile_e[:, :], tile_e_i[:, :])
            V.memset(step16[:, 0:1], -1.0)
            V.tensor_copy(step16[:, 1:NT + 1], iota_i[:, :])
            own(V.tensor_copy(pidx[:, :], pidx_i[:, :]))
            for c in range(NCH):
                own(V.tensor_scalar(pidx_c[:, c:c + 1], pidx[:, :], float(c * CH), None, ALU.add))
            V.tensor_scalar(ident[:, :], iota[:, :], pidx[:, 0:1], None, ALU.is_equal)
            V.tensor_scalar(ident16[:, :], iota[:, :], pidx[:, 0:1], None, ALU.is_equal)
            V.tensor_scalar(before_p[:, :], iota[:, :], pidx[:, 0:1], None, ALU.is_gt)
            V.tensor_scalar(upto_p[:, :], iota[:, :], pidx[:, 0:1], None, ALU.is_ge)
            V.tensor_scalar(before_b[:, :], iota[:, :], pidx[:, 0:1], float(P), ALU.is_gt, ALU.mult)
            for c in range(NCH):
                last = V.tensor_scalar(before_t[:, c, :], iota16[:, 0:EC], pidx_c[:, c:c + 1], None, ALU.is_gt)
            own(last)
            V.sem_inc(s_const, 1)
            V.sem_inc(s_msg, 4)
            V.sem_inc(s_acc, 4)
            V.sem_inc(s_acc1, 8)
            V.sem_inc(s_xtd, 2)

            def norm_stats():
                m_e, m_o = stats[:, :, 1], stats[:, :, 4]
                v_e, v_o = stats[:, :, 2], stats[:, :, 5]

                def one(b, u, i):
                    V.bn_stats(row(stats, b), row(xs, b)).then_inc(s_bn, 1)
                buckets(dve, one)
                norm_stats.calls += 1
                dve.wait_ge(s_bn, NB * norm_stats.calls)
                V.tensor_tensor(mean[:, :], m_e, m_o, ALU.add)
                V.tensor_tensor(half[:, :], m_e, m_o, ALU.subtract)
                own(V.tensor_tensor(var[:, :], v_e, v_o, ALU.add))
                own(V.tensor_tensor(half[:, :], half[:, :], half[:, :], ALU.mult))
                V.tensor_scalar(mean[:, :], mean[:, :], 0.5, None, ALU.mult)
                own(V.tensor_scalar(var[:, :], var[:, :], 1.0 / D, None, ALU.mult))
                V.scalar_tensor_tensor(var[:, :], half[:, :], 0.25, var[:, :], ALU.mult, ALU.add).then_inc(s_var, 1)
                dve.wait_ge(s_std, norm_stats.calls)
                own(V.reciprocal(rstd[:, :], rstd[:, :]))
                V.scalar_tensor_tensor(nmr[:, :], mean[:, :], -1.0, rstd[:, :], ALU.mult, ALU.mult).then_inc(s_ln, 1)
            norm_stats.calls = 0

            a, b_ = ti[0:EP, 0:EC], tj[0:EP, 0:EC]

            def digits(w, link):
                key = e_dst if w == 0 else e_src
                if w == 0:
                    link(V.tensor_copy(a, e_src[:, :]))
                else:
                    link(V.tensor_scalar(a, e_typ[:, :], float(N), None, ALU.mult))
                    link(V.tensor_tensor(a, a, e_dst[:, :], ALU.add))
                link(V.tensor_scalar(b_, a, 4, None, ALU.logical_shift_right))
                V.tensor_copy(dig[w][:, 0, :], b_)
                link(V.tensor_scalar(a, a, 15, 7, ALU.bitwise_and, ALU.logical_shift_left))
                link(V.tensor_scalar(b_, key[:, :], P - 1, None, ALU.bitwise_and))
                link(V.tensor_tensor(a, a, b_, ALU.add))
                link(V.tensor_scalar(dig[w][:, 1, :], a, 1.0, None, ALU.add))

            def tiles_of_buckets(w):
                key = e_dst if w == 0 else e_src
                own(V.tensor_scalar(b_, key[:, :], 7, None, ALU.logical_shift_right))
                own(V.tensor_copy(hi16[:, :], b_))
                for b in range(NB):
                    last = V.tensor_scalar(onehot_b[0:EP, b, :], hi16[:, :], float(b), None, ALU.is_equal)
                last.then_inc(s_oh[w], 1)
                dve.wait_ge(s_cnt[w], 1)
                V.tensor_copy(cntT[0:CH, :, :], bank[6][0:CH, 0:NCH * NB].rearrange("p (c b) -> p c b", b=NB)
                              ).then_inc(s_cntc[w], 1)
                dve.wait_ge(s_tot[w], 1)
                own(V.tensor_scalar(tiles_i[:, :], bank[7][0:NB, 0:1], float(P - 1), None, ALU.add))
                own(V.tensor_scalar(tiles_i[:, :], tiles_i[:, :], 7, None, ALU.logical_shift_right))
                own(V.tensor_scalar(tiles_s[:, :], tiles_i[:, :], float(-P), None, ALU.mult))
                V.tensor_tensor(short[:, :], bank[7][0:NB, 0:1], tiles_s[:, :], ALU.add)
                V.tensor_copy(tiles_f[:, :], tiles_i[:, :]).then_inc(s_tiles[w], 1)
                dve.wait_ge(s_incl[w], 1)
                own(V.tensor_copy(incl[:, :], bank[7][0:NB, 8:9]))
                V.tensor_scalar(passed[:, :], iota16[0:NB, :], incl[:, 0:1], None, ALU.is_ge).then_inc(s_passed[w], 1)
                dve.wait_ge(s_bt[w], 1)
                V.tensor_scalar(bt[w][:, 0:NT], bank[6][:, 0:NT], float(NB - 1), None, ALU.min).then_inc(s_btc[w], 1)

            def places(w, link):
                for b in range(NB):
                    dve.wait_ge(s_rank[w], b + 1)
                    if b:
                        dve.wait_ge(s_rankc[w], b)
                    V.copy_predicated(pos[:, :], onehot_b[0:EP, b, :].bitcast(u16),
                                      bank[4 + b % 2][0:EP, 0:EC]).then_inc(s_rankc[w], 1)
                dve.wait_ge(s_rankc[w], NB)
                link(V.tensor_copy(a, pos[:, :]))
                link(V.tensor_scalar(b_, a, P - 1, None, ALU.bitwise_and))
                V.tensor_copy(plo[w][:, :], b_)
                link(V.tensor_scalar(a, a, 7, None, ALU.logical_shift_right))
                link(V.tensor_scalar(nphi[w][:, :], a, -1.0, 0.5, ALU.mult, ALU.add))

            def place_onehot(w, t, slot, g):
                if g == 0:
                    dve.wait_ge(s_hotu[w], t + 1)
                V.tensor_scalar(Ls[:, slot, g, :], iota16[0:EP, 0:P], plo[w][:, ds(t, 1)],
                                dig[w][:, g, ds(t, 1)], ALU.is_equal, ALU.mult).then_inc(s_L[w], 1)

            def sorted_tiles(w, banks, link):
                dve.wait_ge(s_srt[w], 1)
                for g in range(2):
                    link(V.tensor_copy(srt[:, g, :], bank[banks + g][:, 0:NT + 1]))
                for g in range(2):
                    link(V.tensor_tensor(srt[:, g, 0:NT], srt[:, g, 1:NT + 1], srt[:, g, 0:NT], ALU.subtract))
                link(V.tensor_scalar(srt[:, 1, 0:NT], srt[:, 1, 0:NT], 0.5, None, ALU.mult))
                link(V.tensor_scalar(ti[:, :], srt[:, 1, 0:NT], -1.0, 0.0, ALU.add, ALU.max))
                link(V.tensor_scalar(srt[:, 1, 0:NT], srt[:, 1, 0:NT], 0.0, NO_NODE, ALU.is_equal, ALU.mult))
                link(V.tensor_scalar(tj[:, :], ti[:, :], P - 1, None, ALU.bitwise_and))
                V.tensor_tensor(lof[w][:, 0:NT], srt[:, 1, 0:NT], tj[:, :], ALU.add)
                link(V.tensor_scalar(ti[:, :], ti[:, :], 7, None, ALU.logical_shift_right))
                link(V.scalar_tensor_tensor(idx[w][:, :], srt[:, 0, 0:NT], 8.0, ti[:, :], ALU.mult, ALU.add))

            dve.wait_ge(s_x, 32)
            norm_stats()
            dve.wait_ge(s_wt, 1)
            own(V.tensor_copy(w0T[:, :, 0:D], bank[4][:, :].rearrange("p (j n) -> p j n", j=2)))
            V.tensor_copy(w0T[:, :, D:ZW], bank[5][:, 0:2 * 2 * H].rearrange("p (j n) -> p j n", j=2)).then_inc(s_wtc, 1)

            dve.wait_ge(s_edges, 48)
            digits(1, own)
            tiles_of_buckets(1)
            places(1, own)
            tiles_of_buckets(0)
            dve.wait_ge(s_keyn, 16)
            own(V.tensor_scalar(b_, e_nxt[:, :], 7, None, ALU.logical_shift_right))
            own(V.tensor_copy(hn16[:, :], b_))
            own(V.tensor_tensor(pos[:, :], hn16[:, :], hi16[:, :], ALU.is_lt))
            V.tensor_reduce(drops[:, :], pos[:, :], AX.X, ALU.add).then_inc(s_drop, 1)
            dve.wait_ge(s_dropc, 1)
            own(V.tensor_scalar(sort_it[:, :], bank[5][:, 0:1], 1.0, None, ALU.min))
            V.sem_inc(s_flag, 1)
            dve.wait_ge(s_first, 1)
            own(V.tensor_tensor(first_e[:, :], tile_e[:, :], bank[4][0:TG, 0:NCH], ALU.add))
            own(V.tensor_scalar(first_i[:, :], first_e[:, :], float(E), None, ALU.min))
            own(V.tensor_scalar(tile_b[:, :], bank[4][0:TG, 8:8 + NCH], float(NB - 1), float(P), ALU.min, ALU.mult))
            V.sem_inc(s_firstc, 1)

            dve.wait_ge(s_zc, NB + 2)
            V.tensor_copy(sdm[:, :, 0:H], zall[:, :, D + H:ZW])
            V.tensor_reduce(top[:, :], zall[:, :, D:D + H].rearrange("p b h -> p h b"), AX.X, ALU.max).then_inc(s_top, 1)
            dve.wait_ge(s_topa, 1)
            own(V.tensor_tensor(tmp_m[:, :, :], zall[:, :, D + H:ZW],
                                top_all[:, :].rearrange("p (a h) -> p a h", a=1).to_broadcast((P, NB, H)), ALU.add))
            own(V.scalar_tensor_tensor(sdm[:, :, H:2 * H], tmp_m[:, :, :], SLOPE, tmp_m[:, :, :], ALU.mult, ALU.max))
            V.sem_inc(s_sdm, 1)

            grouped = dve.value_load(sort_it[0:1, 0:1], min_val=0, max_val=1)
            with dve.If(grouped < 1):
                dve.wait_ge(s_slices, 16 * 2 * NCH)
                slow = Chain(dve, slow_own)
                for c in range(NCH):
                    V.tensor_scalar(keyF[:, c, :], keyT[:, c, :], tile_b[:, c:c + 1], None, ALU.subtract)
                slow(V.tensor_copy(rowF[:, :, :], rowT[:, :, :]))
                V.sem_inc(s_tl, 1)
                dve.wait_ge(s_tt, 1)
                V.tensor_copy(lof[0][:, 0:NT], bank[4][:, 0:NT])
                slow(V.tensor_copy(idx[0][:, :], bank[5][:, 0:NT]))
            with dve.If(grouped > 0):
                slow = Chain(dve, slow_own)
                digits(0, slow)
                V.sem_inc(s_sorting, 1)
                places(0, slow)
                V.sem_inc(s_sorting, 1)
                with dve.Fori(0, EC // K) as i:
                    for k in range(K):
                        for g in range(2):
                            place_onehot(0, i * K + k, k, g)
                sorted_tiles(0, 4, slow)
            V.sem_inc(s_sorted[0], 1)

            def onehots(w, t0, into, done):
                V.tensor_tensor(into, iota[:, :].rearrange("p (a n) -> p a n", a=1).to_broadcast((P, K, P)),
                                lof[w][:, ds(t0, K)].rearrange("p (k a) -> p k a", a=1).to_broadcast((P, K, P)),
                                ALU.is_equal).then_inc(done, 1)

            dve.wait_ge(s_acc0z, 1)
            onehots(0, 0, Ob[:, :, :], s_O)
            with dve.Fori(0, NBATCH // 2) as i:
                own.enter(i, 6)
                for s in range(2):
                    t0 = i * 2 * K + s * K
                    g = G[:, s * K:(s + 1) * K, :]
                    scores = bank[1][:, 0:K * 2 * H].rearrange("p (k c) -> p k c", k=K)
                    dve.wait_ge(s_sd, i * 2 + (s + 1))
                    for j in range(K):
                        dve.wait_ge(s_g[s * K + j], i * 16 + 16)
                    own(V.tensor_tensor(ev[:, :, :], g[:, :, D:D + H], scores[:, :, 0:H], ALU.add))
                    own(V.scalar_tensor_tensor(ev2[:, :, :], ev[:, :, :], SLOPE, ev[:, :, :], ALU.mult, ALU.max))
                    own(V.tensor_tensor(ev[:, :, :], ev2[:, :, :], scores[:, :, H:2 * H], ALU.subtract))
                    V.tensor_scalar(ev[:, :, :], ev[:, :, :], 0.0, None, ALU.min).then_inc(s_ev, 1)
                    onehots(0, t0 + K, Ob[:, :, :], s_O)
                    dve.wait_ge(s_ex, i * 2 + (s + 1))
                    for q in range(2):
                        ks = slice(q * K // 2, (q + 1) * K // 2)
                        V.tensor_tensor(msg[:, ks, 0:D].rearrange("p k (h d) -> p k h d", h=H),
                                        g[:, ks, 0:D].rearrange("p k (h d) -> p k h d", h=H),
                                        msg[:, ks, D:MW].rearrange("p k (h a) -> p k h a", a=1).to_broadcast((P, K // 2, H, DH)),
                                        ALU.mult).then_inc(s_msg, 1)
                    buckets_of = load_buckets(dve, f"dve0{s}", 0, t0)
                    for k in range(K):
                        b = buckets_of[k]
                        dve.wait_ge(s_agg, t0 + (k + 1))
                        dve.wait_ge(s_acc, t0 + (k + 4))
                        V.tensor_tensor(row(acc0, b), row(acc0, b), bank[2 + k % 4][:, 0:MW], ALU.add).then_inc(s_acc, 1)
                        if k // 2 < C0:
                            place_onehot(1, i * 2 * C0 + (s * C0 + k // 2), s * C0 + k // 2, k % 2)
                own.leave(6, NBATCH // 2)

            dve.wait_ge(s_acc, NT + 4)
            own(V.tensor_scalar(rden[:, :, :], acc0[:, :, D:MW], 1e-9, None, ALU.max))
            own(V.reciprocal(rden[:, :, :], rden[:, :, :]))

            with dve.Fori(0, NB) as b:
                own.enter(b, 1)
                q = row(acc0, b)[:, 0:D].rearrange("p (h d) -> p h d", h=H)
                own(V.tensor_tensor(q, q, row(rden, b).rearrange("p (h a) -> p h a", a=1).to_broadcast((P, H, DH)), ALU.mult))
                V.tensor_tensor(row(xs, b), row(xs, b), row(acc0, b)[:, 0:D], ALU.add).then_inc(s_x1, 1)
                own.leave(1, NB)
            dve.wait_ge(s_x1, NB)
            norm_stats()
            dve.wait_ge(s_bias, 16)
            V.tensor_copy(acc1, bias_b[:, :].rearrange("p (a d) -> p a d", a=1).to_broadcast((P, NB, D))).then_inc(s_acc1z, 1)

            def copy_hT(b, u, i):
                dve.wait_ge(s_hT, b + (NB + 3))
                V.tensor_copy(hT[:, u, :, :].rearrange("p j n -> p (j n)"), bank[u][:, 0:D]).then_inc(s_hTc, 1)

            def copy_xt(b, u, i):
                if not isinstance(b, int):
                    for k in range(C1):
                        for g in range(2):
                            place_onehot(1, i * 2 * C1 + (u * C1 + k + C0 * NBATCH), k, g)
                dve.wait_ge(s_stage, b + 1)
                for c in range(2):
                    dve.wait_ge(s_xt, b * 4 + (c + 3))
                    V.tensor_copy(stage[:, u, (c + 2) * 512:(c + 3) * 512], bank[4 + c][:, :]).then_inc(s_xtd, 1)
            buckets(dve, copy_hT, copy_xt)
            sorted_tiles(1, 6, own)
            V.sem_inc(s_sorted[1], 1)

            dve.wait_ge(s_acc1z, 1)
            onehots(1, 0, O[:, 0:K, :], s_O1)
            with dve.Fori(0, NBATCH // 2) as i:
                for s in range(2):
                    t0 = i * 2 * K + s * K
                    onehots(1, t0 + K, O[:, (1 - s) * K:(2 - s) * K, :], s_O1)
                    buckets_of = load_buckets(dve, f"dve1{s}", 1, t0)
                    for k in range(K):
                        b = buckets_of[k]
                        dve.wait_ge(s_agg1, t0 + (k + 1 + 2 * K))
                        dve.wait_ge(s_acc1, t0 + (k + 8))
                        r = acc1[:, ds(b, 1), :].rearrange("p b d -> p (b d)")
                        V.tensor_tensor(r, r, bank[k][:, 0:D], ALU.add).then_inc(s_acc1, 1)

            dve.wait_ge(s_acc1, NT + 8)
            with dve.Fori(0, NB // FC) as c:
                r = acc1[:, ds(c * FC, FC), :]
                q = xs[:, ds(c * FC, FC), :]
                V.scalar_tensor_tensor(q, r, 0.0, q, ALU.max, ALU.add).then_inc(s_fin, 1)

        @block.scalar
        def _(act):
            A = nc.scalar
            A.sem_inc(s_xta, 2)
            A.sem_inc(s_zc, 2)

            def norm(w):
                act.wait_ge(s_var, w + 1)
                A.activation(rstd[:, :], var[:, :], ACT.Sqrt, bias=epst[:, 0:1]).then_inc(s_std, 1)
                act.wait_ge(s_ln, w + 1)

            def make_h(base):
                def one(b, u, i):
                    act.wait_ge(s_hT, b + (base + 1))
                    A.activation(hn[:, u, :], row(xs, b), ACT.Relu, bias=nmr[:, ds(b, 1)], scale=rstd[:, ds(b, 1)]
                                 ).then_inc(s_h, 1)
                return one

            def tile_step(w, t, slot):
                act.wait_ge(s_hotu[w], t + 1)
                A.activation(Hs[:, slot, 0:NT + 1], step16[0:EP, :], ACT.Sign, bias=nphi[w][:, ds(t, 1)]).then_inc(s_H[w], 1)

            act.wait_ge(s_const, 1)
            norm(0)

            def copy_hT(b, u, i):
                act.wait_ge(s_hT, b + 3)
                A.copy(hT[:, u, :, :].rearrange("p j n -> p (j n)"), bank[u][:, 0:D]).then_inc(s_hTc, 1)

            def copy_z(b, u, i):
                act.wait_ge(s_z, b + 1)
                A.copy(row(zall, b), bank[2 + u][:, 0:ZW]).then_inc(s_zc, 1)
            buckets(act, make_h(0), copy_hT, copy_z)

            act.wait_ge(s_flag, 1)
            with act.If(act.value_load(sort_it[0:1, 0:1], min_val=0, max_val=1) > 0):
                act.wait_ge(s_sorting, 2)
                with act.Fori(0, EC // K) as i:
                    for k in range(K):
                        tile_step(0, i * K + k, k)

            def turned(batch, half_):
                act.wait_ge(s_O, batch + 1)
                A.copy(O[:, half_ * K:(half_ + 1) * K, :].rearrange("p k n -> p (k n)"),
                       Ob[:, :, :].rearrange("p k n -> p (k n)")).then_inc(s_O32, 1)
                act.wait_ge(s_Ot, batch + 1)
                A.copy(OT[:, :, :].rearrange("p k e -> p (k e)"), bank[0][:, :].bitcast(bf16)).then_inc(s_OTc, 1)
            turned(0, 0)
            with act.Fori(0, NBATCH // 2) as i:
                for s in range(2):
                    act.wait_ge(s_ev, i * 2 + (s + 1))
                    A.activation(msg[:, :, D:MW], ev[:, :, :], ACT.Exp).then_inc(s_ex, 1)
                    turned(i * 2 + (s + 1), 1 - s)
                    for c in range(C0):
                        tile_step(1, i * 2 * C0 + (s * C0 + c), s * C0 + c)

            norm(1)
            def copy_xt(b, u, i):
                act.wait_ge(s_stage, b + 1)
                if not isinstance(b, int):
                    for k in range(C1):
                        tile_step(1, i * 2 * C1 + (u * C1 + k + C0 * NBATCH), k)
                for c in range(2):
                    act.wait_ge(s_xt, b * 4 + (c + 1))
                    A.copy(stage[:, u, c * 512:(c + 1) * 512], bank[2 + c][:, :]).then_inc(s_xta, 1)
            buckets(act, make_h(NB), copy_xt)

        @block.tensor
        def _(pe):
            T = nc.tensor
            T.sem_inc(s_hT, 2)
            T.sem_inc(s_hTc, 2)
            for w in range(2):
                T.sem_inc(s_hotu[w], K)
            T.sem_inc(s_agg1, 2 * K)
            pe.wait_ge(s_const, 1)
            pe.wait_ge(s_w0, 16)
            pe.wait_ge(s_attn, 16 * 8)
            for k in range(2):
                for j in range(2):
                    T.transpose(bank[4][:, (k * 2 + j) * P:(k * 2 + j + 1) * P], w_rows[:, j, k * P:(k + 1) * P], ident[:, :])
            for k in range(2):
                for j in range(2):
                    last = T.matmul(bank[5][:, k * 2 * H:(k + 1) * 2 * H], w_rows[:, j, k * P:(k + 1) * P],
                                    attn_cols[:, j, :], start=(j == 0), stop=(j == 1))
            last.then_inc(s_wt, 1)

            def turn_h(base):
                def one(b, u, i):
                    pe.wait_ge(s_h, b + (base + 1))
                    pe.wait_ge(s_hTc, b + (base + 1))
                    for j in range(2):
                        last = T.transpose(bank[u][:, j * P:(j + 1) * P], hn[:, u, j * P:(j + 1) * P], ident[:, :])
                    last.then_inc(s_hT, 1)
                return one

            pe.wait_ge(s_wtc, 1)
            def layer0_table(b, u, i):
                pe.wait_ge(s_hTc, b + 3)
                pe.wait_ge(s_zc, b + 1)
                for j in range(2):
                    last = T.matmul(bank[2 + u][:, 0:ZW], hT[:, u, j, :], w0T[:, j, :], start=(j == 0), stop=(j == 1))
                last.then_inc(s_z, 1)
            buckets(pe, turn_h(0), layer0_table)

            def tiles_of_buckets(w):
                pe.wait_ge(s_oh[w], 1)
                for c in range(NCH):
                    for b in range(NB):
                        last = T.matmul(bank[6][0:CH, c * NB + b:c * NB + b + 1], onehot_b[0:EP, b, c * CH:(c + 1) * CH],
                                        ones16[0:EP, 0:1], start=True, stop=True)
                last.then_inc(s_cnt[w], 1)
                pe.wait_ge(s_cntc[w], 1)
                for c in range(NCH):
                    last = T.matmul(bank[7][0:NB, 0:1], cntT[0:CH, c, :], ones16[0:CH, 0:1], start=(c == 0), stop=(c == NCH - 1))
                last.then_inc(s_tot[w], 1)
                pe.wait_ge(s_tiles[w], 1)
                T.matmul(bank[7][0:NB, 8:9], upto_p[0:NB, 0:NB], tiles_f[:, :], start=True, stop=True).then_inc(s_incl[w], 1)
                pe.wait_ge(s_passed[w], 1)
                T.matmul(bank[6][:, 0:NT], ones16[0:NB, :], passed[:, :], start=True, stop=True).then_inc(s_bt[w], 1)

            def places(w):
                for b in range(NB):
                    if b >= 2:
                        pe.wait_ge(s_rankc[w], b - 1)
                    o = bank[4 + b % 2][0:EP, 0:EC]
                    T.matmul(o, before_p[0:EP, 0:EP], onehot_b[0:EP, b, :], start=True, stop=False)
                    for c in range(NCH):
                        T.matmul(o, cntT[0:CH, c, b:b + 1].to_broadcast((CH, EP)), before_t[0:CH, c, :], start=False, stop=False)
                    T.matmul(o, tiles_f[:, 0:1].to_broadcast((NB, EP)), before_b[0:NB, b:b + 1].to_broadcast((NB, EC)),
                             start=False, stop=True).then_inc(s_rank[w], 1)

            def open_sums(banks):
                for g in range(2):
                    T.matmul(bank[banks + g][:, 0:NT + 1], zeros16[0:EP, 0:P], zeros16[0:EP, :], start=True, stop=False)

            def sort_column(w, banks, t, slot):
                pe.wait_ge(s_L[w], t * 2 + 2)
                pe.wait_ge(s_H[w], t + 1)
                for g in range(2):
                    last = T.matmul(bank[banks + g][:, 0:NT + 1], Ls[:, slot, g, :], Hs[:, slot, 0:NT + 1], start=False, stop=False)
                last.then_inc(s_hotu[w], 1)

            def close_sums(banks, w):
                for g in range(2):
                    last = T.matmul(bank[banks + g][:, 0:NT + 1], zeros16[0:EP, 0:P], zeros16[0:EP, :], start=False, stop=True)
                last.then_inc(s_srt[w], 1)

            tiles_of_buckets(1)
            places(1)
            tiles_of_buckets(0)
            pe.wait_ge(s_drop, 1)
            T.matmul(bank[5][:, 0:1], ones_f[:, :], drops[:, :], start=True, stop=True).then_inc(s_dropc, 1)
            for c in range(NCH):
                T.matmul(bank[4][0:TG, c:c + 1], passed[:, c * TG:(c + 1) * TG], short[:, :], start=True, stop=True)
                last = T.matmul(bank[4][0:TG, 8 + c:9 + c], passed[:, c * TG:(c + 1) * TG], ones16[0:NB, 0:1],
                                start=True, stop=True)
            last.then_inc(s_first, 1)
            pe.wait_ge(s_flag, 1)
            pe.wait_ge(s_firstc, 1)
            grouped = pe.value_load(sort_it[0:1, 0:1], min_val=0, max_val=1)
            with pe.If(grouped < 1):
                pe.wait_ge(s_tl, 1)
                for c in range(NCH):
                    T.transpose(bank[4][:, c * TG:(c + 1) * TG], keyF[:, c, :], ident[0:TG, 0:TG])
                    last = T.transpose(bank[5][:, c * TG:(c + 1) * TG], rowF[:, c, :], ident[0:TG, 0:TG])
                last.then_inc(s_tt, 1)
            with pe.If(grouped > 0):
                pe.wait_ge(s_sorting, 1)
                places(0)
                pe.wait_ge(s_rankc[0], NB)
                open_sums(4)
                with pe.Fori(0, EC // K) as i:
                    for k in range(K):
                        sort_column(0, 4, i * K + k, k)
                close_sums(4, 0)

            def turn_onehots(batch):
                pe.wait_ge(s_O, batch + 1)
                for k in range(K):
                    last = T.transpose(bank[0][:, :].bitcast(bf16)[:, k * P:(k + 1) * P], Ob[:, k, :], ident16[:, :])
                last.then_inc(s_Ot, 1)

            def scores(name, batch, t0):
                buckets_of = load_buckets(pe, f"pe{name}", 0, t0)
                pe.wait_ge(s_OTc, batch + 1)
                for k in range(K):
                    last = T.matmul(bank[1][:, k * 2 * H:(k + 1) * 2 * H], OT[:, k, :], row(sdm, buckets_of[k]),
                                    start=True, stop=True)
                last.then_inc(s_sd, 1)

            open_sums(6)
            pe.wait_ge(s_btc[0], 1)
            pe.wait_ge(s_sdm, 1)
            turn_onehots(0)
            scores("first", 0, 0)
            with pe.Fori(0, NBATCH // 2) as i:
                for s in range(2):
                    t0 = i * 2 * K + s * K
                    turn_onehots(i * 2 + (s + 1))
                    pe.wait_ge(s_O32, i * 2 + (s + 1))
                    for k in range(K):
                        if k % 4 == 0:
                            pe.wait_ge(s_msg, i * 4 + (2 * s + k // 4 + 5))
                        pe.wait_ge(s_acc, t0 + (k + 1))
                        T.matmul(bank[2 + k % 4][:, 0:MW], O[:, s * K + k, :], msg[:, k, :], start=True, stop=True).then_inc(s_agg, 1)
                    pe.wait_ge(s_ev, i * 2 + (s + 1))
                    scores(s, i * 2 + (s + 1), t0 + K)
                    for c in range(C0):
                        sort_column(1, 6, i * 2 * C0 + (s * C0 + c), s * C0 + c)

            pe.wait_ge(s_w1, 32)
            def layer1_table(b, u, i):
                pe.wait_ge(s_hTc, b + (NB + 3))
                for c in range(4):
                    pe.wait_ge(s_xta if c < 2 else s_xtd, b * 2 + (c % 2 + 1))
                    for q in range(2):
                        for j in range(2):
                            last = T.matmul(bank[2 + c][:, q * D:(q + 1) * D], hT[:, u, j, :], w1s[:, j, 2 * c + q, :],
                                            start=(j == 0), stop=(j == 1))
                    last.then_inc(s_xt, 1)
                if not isinstance(b, int):
                    for k in range(C1):
                        sort_column(1, 6, i * 2 * C1 + (u * C1 + k + C0 * NBATCH), k)
            buckets(pe, turn_h(NB), layer1_table)
            close_sums(6, 1)
            pe.wait_ge(s_sorted[1], 1)

            with pe.Fori(0, NBATCH // 2) as i:
                for s in range(2):
                    t0 = i * 2 * K + s * K
                    pe.wait_ge(s_O1, i * 2 + (s + 1))
                    for k in range(K):
                        pe.wait_ge(s_g[s * K + k], i * 16 + 16 * (NBATCH // 2 + 1))
                        pe.wait_ge(s_acc1, t0 + (k + 1))
                        T.matmul(bank[k][:, 0:D], O[:, s * K + k, :], G[:, s * K + k, 0:D], start=True, stop=True).then_inc(s_agg1, 1)


_INS = ['x', 'src', 'dst', 'edge_type_8', 'L0_gnn_W', 'L0_gnn_attn', 'L1_gnn_weight', 'L1_gnn_bias']
_OUTS = [((N, D), 'float32')]


def kernel(**inputs):
    import numpy as _np
    import concourse.bacc as _bacc
    from concourse import mybir as _mybir
    from concourse.bass_utils import run_bass_kernel_spmd as _run

    nc = _bacc.Bacc("TRN2", target_bir_lowering=False, num_devices=1)
    arrays, args = {}, []
    for name in _INS:
        a = _np.ascontiguousarray(inputs[name])
        arrays[f"in_{name}_dram"] = a
        args.append(nc.dram_tensor(f"in_{name}_dram", a.shape, _mybir.dt.from_np(a.dtype), kind="ExternalInput").ap())
    for i, (shape, dtype) in enumerate(_OUTS):
        dt = _mybir.dt.from_np(_np.dtype(dtype))
        args.append(nc.dram_tensor(f"out_{i}_dram", shape, dt, kind="ExternalOutput").ap())
    build(nc, *args)
    r = _run(nc, [arrays], core_ids=[0])
    return r.results[0]["out_0_dram"]
```

```python
import concourse.bass as bass
from concourse import mybir
from contextlib import ExitStack

P = 128
N, E, D = 3125, 50000, 256
H, DH, R = 4, 64, 8
NB = -(-N // P)
NBP = NB + 1
EP, EC = 125, 400
NT = 416
CH, NCH = 100, 4
ZW = D + 2 * H
MW = D + H
K = 8
NBATCH = NT // K
XC = 4
FC = 5
C0, C1 = 5, 5
CL = EC - C0 * NBATCH - C1 * (NB - 1)
S = 2 * C0
RANK_BANKS = (4, 5, 2, 3)
TG = NT // NCH
EPS = 1e-5
SLOPE = 0.01
NO_NODE = -200.0
NO_SCORE = -1e30
MAX_SPREAD = 16.0

assert EP * EC == E and CH * NCH == EC and E // P + NB <= NT < E // P + NB + 2 * K and NB % FC == 0 and NB % 2 == 1 and NBATCH % 2 == 0
assert C0 == C1 == 5 and CL > 0 and CL % S == 0 and EC % S == 0


class Chain:

    def __init__(self, eng, sem):
        self.eng, self.sem, self.n, self.off = eng, sem, 0, 0

    def __call__(self, ins):
        ins.then_inc(self.sem, 1)
        self.n += 1
        self.eng.wait_ge(self.sem, self.off + self.n)

    def enter(self, i, per):
        self.off = i * per
        self.start = self.n

    def leave(self, per, trips):
        assert self.n - self.start == per, (self.n - self.start, per)
        self.off = 0
        self.n = self.start + per * trips


def build(nc, x, src, dst, etype, w0, attn, w1, bias, out):
    f32, f16, bf16, i32, u16 = (mybir.dt.float32, mybir.dt.float16, mybir.dt.bfloat16, mybir.dt.int32,
                                mybir.dt.uint16)
    ALU, ACT, AX = mybir.AluOpType, mybir.ActivationFunctionType, mybir.AxisListType
    ds = bass.ds

    with ExitStack() as ctx:
        def sb(name, shape, dt=f32):
            return ctx.enter_context(nc.sbuf_tensor(name, shape, dt))

        def sem(name):
            return ctx.enter_context(nc.semaphore(name))

        z_table = nc.dram_tensor("z_table", (NB * P, ZW), f32, kind="Internal").ap()
        xt_table = nc.dram_tensor("xt_table", (R * N, D), f32, kind="Internal").ap()
        key_pad = nc.dram_tensor("key_pad", (E + P,), i32, kind="Internal").ap()
        row_pad = nc.dram_tensor("row_pad", (E + P,), i32, kind="Internal").ap()

        iota_i = sb("iota_i", [P, NT], i32)
        pidx_i = sb("pidx_i", [P, 1], i32)
        iota = sb("iota", [P, P])
        iota16 = sb("iota16", [P, NT], f16)
        pidx = sb("pidx", [P, 1])
        pidx_c = sb("pidx_c", [P, NCH])
        ident = sb("ident", [P, P])
        ones16 = sb("ones16", [P, P], f16)
        zeros16 = sb("zeros16", [P, NT + 1], f16)
        ident16 = sb("ident16", [P, P], bf16)
        ones_f = sb("ones_f", [EP, P])
        step16 = sb("step16", [P, NT + 1], f16)
        tile_e = sb("tile_e", [TG, NCH])
        tile_e_i = sb("tile_e_i", [TG, NCH], i32)
        pads = sb("pads", [1, 2, P], i32)
        before_p = sb("before_p", [P, P], f16)
        upto_p = sb("upto_p", [P, P], f16)
        before_t = sb("before_t", [P, NCH, EC], f16)
        part_b = sb("part_b", [32 + NB, NB], f16)
        pidx_32 = sb("pidx_32", [P, 1])
        before_b = sb("before_b", [P, P], f16)

        G = sb("G", [P, 2 * K, ZW])
        G_flat = G[:, :, :].rearrange("p k z -> p (k z)")
        w1s = G_flat[:, 0:2 * R * D].rearrange("p (j r o) -> p j r o", j=2, r=R)

        xs = sb("xs", [P, NBP, D])
        hn = sb("hn", [P, 2, D])
        hT = sb("hT", [P, 2, 2, P])
        zall = sb("zall", [P, NB, ZW])
        acc0 = sb("acc0", [P, NBP, MW])
        acc1 = zall[:, :, 0:D]
        stats = sb("stats", [P, NBP, 6])
        mean = sb("mean", [P, NBP])
        var = sb("var", [P, NBP])
        half = sb("half", [P, NBP])
        rstd = sb("rstd", [P, NBP])
        nmr = sb("nmr", [P, NBP])
        epst = sb("epst", [P, 1])
        sdm = sb("sdm", [P, NB, 2 * H])
        top = sb("top", [P, 2 * H])
        top_all = sb("top_all", [P, 2 * H])
        spread = sb("spread", [P, H])
        spread_it = sb("spread_it", [P, 1], i32)
        tmp_m = sb("tmp_m", [P, NB, H])
        rden = sb("rden", [P, NBP, H])
        w_rows = sb("w_rows", [P, 2, D])
        attn_cols = sb("attn_cols", [P, 2, 2 * H])
        w0T = sb("w0T", [P, 2, ZW])
        bias_b = sb("bias_b", [P, D])

        e_src = sb("e_src", [EP, EC], i32)
        e_dst = sb("e_dst", [EP, EC], i32)
        e_typ = sb("e_typ", [EP, EC], i32)
        Hs = sb("Hs", [EP, S, NT + 2], f16)
        Ls = sb("Ls", [EP, S, 2, P], f16)
        Hs_i = Hs[:, :, :].rearrange("p k t -> p (k t)").bitcast(i32)
        e_nxt = Ls[:, :, :, :].rearrange("p k g n -> p (k g n)").bitcast(i32)[:, 0:EC]
        ti = sb("ti", [P, NT], i32)
        tj = sb("tj", [P, NT], i32)
        pos = sb("pos", [EP, EC])
        hi16 = sb("hi16", [EP, EC], f16)
        hn16 = sb("hn16", [EP, EC], f16)
        drops = sb("drops", [EP, 1])
        sort_it = sb("sort_it", [P, 1], i32)
        plo = [G_flat[0:EP, 0:EC], sb("plo1", [EP, EC])]
        nphi = [G_flat[0:EP, EC:2 * EC], sb("nphi1", [EP, EC])]
        dig = [G_flat[0:EP, 2 * EC:4 * EC].rearrange("p (g t) -> p g t", g=2), sb("dig1", [EP, 2, EC])]
        scratch = sb("scratch", [P, NB * EC // 2])
        onehot_b = scratch[:, :].bitcast(f16).rearrange("p (b t) -> p b t", t=EC)
        stage = scratch[:, 0:2 * R * D].rearrange("p (s n) -> p s n", s=2)
        cntT = sb("cntT", [P, NCH, NB], f16)
        tiles_i = sb("tiles_i", [NB, 1], i32)
        tiles_f = sb("tiles_f", [NB, 1], f16)
        tiles_s = sb("tiles_s", [NB, 1])
        short = sb("short", [NB, 1], f16)
        incl = sb("incl", [NB, 1])
        passed = sb("passed", [NB, NT], f16)
        base = sb("base", [32 + NB, EC], f16)
        base_i = Hs_i[0:NB, 0:EC]
        first_e = sb("first_e", [TG, NCH])
        first_i = sb("first_i", [TG, NCH], i32)
        tile_b = sb("tile_b", [TG, NCH])
        keyT, rowT = (Hs_i[0:TG, n * NCH * P:(n + 1) * NCH * P].rearrange("p (c e) -> p c e", c=NCH) for n in range(2))
        keyF = keyT[:, :, :].bitcast(f32)
        rowF = rowT[:, :, :].bitcast(f32)
        srt = sb("srt", [P, 2, NT + 1])
        idx = [sb(f"idx{w}", [P, NT], i32) for w in range(2)]
        lof = [sb(f"lof{w}", [P, NT + 2 * K]) for w in range(2)]
        bt = [sb(f"bt{w}", [P, NT + K], i32) for w in range(2)]

        O = sb("O", [P, 2 * K, P])
        Ob = sb("Ob", [P, K, P], bf16)
        OT = sb("OT", [P, K, P])
        msg = scratch[:, 0:K * MW].rearrange("p (k m) -> p k m", k=K)
        idx_now = sb("idx_now", [P, 2 * K], i32)
        ev = sb("ev", [P, K, H])
        ev2 = sb("ev2", [P, K, H])

        bank = [ctx.enter_context(nc.psum_tensor(f"bank{i}", [P, 512], f32)) for i in range(8)]

        s_xlast, s_xpad, s_dst, s_edges, s_w0, s_attn, s_azero, s_w1, s_bias = (
            sem(n) for n in ("x_last_in", "x_pad", "targets_in", "edges_in", "w0_in", "attn_in", "attn_zeroed", "w1_in", "bias_in"))
        s_x = [sem(f"x_in{c}") for c in range(XC)]
        s_iota, s_const = sem("iota_made"), sem("consts_made")
        dve_own, pool_own = sem("dve_own"), sem("pool_own")
        def per_sort(name):
            return [sem(f"{name}{w}") for w in range(2)]
        s_oh, s_cnt, s_cntc, s_tot, s_tiles, s_incl, s_passed, s_bt, s_btc = (
            per_sort(n) for n in ("onehots_made", "counts_summed", "counts_copied", "totals_summed", "tiles_made",
                                  "incl_summed", "passed_made", "bt_summed", "bt_copied"))
        s_base, s_based = per_sort("base_summed"), per_sort("base_split")
        s_rank, s_rankc, s_L, s_H, s_hotu, s_srt, s_sorted = (
            per_sort(n) for n in ("rank_summed", "rank_taken", "place_onehots", "tile_steps", "columns_sorted",
                                  "sort_summed", "tiles_sorted"))
        s_key, s_keyn, s_padk = sem("keys_padded"), sem("next_keys_in"), sem("pad_made")
        s_drop, s_dropc, s_flag = sem("drops_counted"), sem("drops_summed"), sem("sort_flag")
        s_first, s_firstc, s_slices, s_tl, s_tt = (
            sem(n) for n in ("first_summed", "first_made", "slices_in", "slices_local", "slices_turned"))
        s_sorting = sem("places_made")
        slow_own, slices_own, turned_own = sem("dve_own_in_sort"), sem("dve_own_in_slices"), sem("dve_own_in_turned")
        s_wt, s_wtc = sem("w0_turned"), sem("w0_turned_copied")
        s_var, s_std, s_ln = sem("var_ready"), sem("std_ready"), sem("ln_ready")
        s_h, s_hT, s_hTc, s_z, s_zc, s_zout = (
            sem(n) for n in ("h_ready", "h_turned", "h_turned_copied", "z_summed", "z_copied", "z_stored"))
        s_top, s_topa, s_sdm, s_acc0z = sem("top_ready"), sem("top_all_ready"), sem("sdm_ready"), sem("acc_zeroed")
        s_g = [sem(f"gathered{j}") for j in range(2 * K)]
        s_O32 = sem("onehot_f32")
        s_O, s_Ot, s_OTc, s_sd, s_ev, s_ex, s_msg, s_agg, s_acc = (
            sem(n) for n in ("onehot_n", "onehot_turned", "onehot_turned_copied", "scores_summed", "logits_ready",
                             "weights_ready", "msg_ready", "agg_summed", "agg_taken"))
        s_stage = sem("stage_free")
        s_xt, s_xta, s_xtd = sem("xt_summed"), sem("xt_copied_act"), sem("xt_copied_dve")
        s_xtout = [sem(f"xt_stored{u}") for u in range(2)]
        s_O1, s_agg1, s_acc1 = sem("onehot1"), sem("agg1_summed"), sem("agg1_taken")
        s_turn = sem("gather_turn")
        s_spread = sem("spread_ready")
        max_own, s_mfree, s_midx, s_min, s_mdiag, s_mspread = (
            sem(n) for n in ("dve_own_in_max", "max_free", "max_idx_copied", "max_rows_in", "max_onehots", "max_rows_spread"))
        s_fin, s_out = sem("rows_final"), sem("out_stored")
        s_acc1z = sem("acc1_from_bias")

        def row(t, b):
            return t[:, ds(b, 1), :].rearrange("p b d -> p (b d)")

        def buckets(eng, *steps):
            with eng.Fori(0, NB // 2) as i:
                for step in steps:
                    for u in range(2):
                        step(i * 2 + u, u, i)
            for step in steps:
                step(NB - 1, 0, NB // 2)

        block = ctx.enter_context(nc.Block())
        full = (N // P) * P
        rest = N - full

        @block.sync
        def _(sp):
            sp.sem_inc(s_stage, 2)
            def columns(a):
                return a.rearrange("(p t) -> p t", t=EC)
            sp.dma_start(e_dst[:, :], columns(dst)).then_inc(s_dst, 16)
            sp.wait_ge(s_padk, 1)
            for a, (pad, arr) in enumerate(((key_pad, dst), (row_pad, src))):
                sp.dma_start(columns(pad[0:E]), columns(arr)).then_inc(s_key, 16)
                sp.dma_start(pad[E:E + P].rearrange("(a p) -> a p", a=1), pads[:, a, :]).then_inc(s_key, 16)
            for c in range(XC):
                at = slice(c * (NB - 1) // XC, (c + 1) * (NB - 1) // XC)
                sp.dma_start(xs[:, at, :], x[at.start * P:at.stop * P, :].rearrange("(b p) d -> p b d", p=P)).then_inc(s_x[c], 16)
            sp.wait_ge(s_key, 64)
            sp.dma_start(e_nxt[:, :], columns(key_pad[1:E + 1])).then_inc(s_keyn, 16)
            sp.wait_ge(s_xpad, 1)
            sp.dma_start(xs[0:rest, NB - 1, :], x[full:N, :]).then_inc(s_xlast, 16)
            for tile, arr in ((e_src, src), (e_typ, etype)):
                sp.dma_start(tile[:, :], columns(arr)).then_inc(s_edges, 16)
            sp.dma_start(w_rows[:, :, :], w0.rearrange("(j a) o d -> (a o) j d", a=2)).then_inc(s_w0, 16)
            sp.wait_ge(s_azero, 1)
            for j in range(2):
                for a in range(2):
                    for s in range(2):
                        c = s * H + 2 * j + a
                        sp.dma_start(attn_cols[a * DH:(a + 1) * DH, j, c:c + 1],
                                     attn[0:1, s * DH:(s + 1) * DH].rearrange("a d -> d a")).then_inc(s_attn, 16)
            sp.dma_start(bias_b[:, :], bias.rearrange("(a d) -> a d", a=1).to_broadcast((P, D))).then_inc(s_bias, 16)

            def store_z(b, u, i):
                sp.wait_ge(s_zc, b + 3)
                sp.dma_start(z_table[ds(b * P, P), :], row(zall, b)).then_inc(s_zout, 16)
            buckets(sp, store_z)

            sp.wait_ge(s_msg, 4 + 2 * NBATCH)
            for j in range(2):
                sp.dma_start(w1s[:, j, :, :], w1[:, j * P:(j + 1) * P, :].rearrange("r p o -> p r o")).then_inc(s_w1, 16)

            xt_v = xt_table.rearrange("(r n) d -> n r d", n=N)

            def store_xt(b, u, i):
                rows = rest if isinstance(b, int) else P
                sp.wait_ge(s_xta, 2 * b + 4)
                sp.wait_ge(s_xtd, 2 * b + 4)
                sp.dma_start(xt_v[ds(b * P, rows), :, :],
                             stage[0:rows, u, :].rearrange("p (r d) -> p r d", r=R)).then_inc(s_xtout[u], 16)
                sp.wait_ge(s_xtout[u], i * 16 + 16)
                sp.sem_inc(s_stage, 1)
            buckets(sp, store_xt)

            out_v = out[0:full, :].rearrange("(b p) d -> p b d", p=P)
            for c in range(NB // FC):
                sp.wait_ge(s_fin, c + 1)
                n = min(FC, NB - 1 - c * FC)
                sp.dma_start(out_v[:, c * FC:c * FC + n, :], xs[:, c * FC:c * FC + n, :]).then_inc(s_out, 16)
            sp.dma_start(out[full:N, :], xs[0:rest, NB - 1, :]).then_inc(s_out, 16)
            sp.wait_ge(s_out, 16 * (NB // FC + 1))

        @block.gpsimd
        def _(pool):
            pool.iota(iota_i[:, :], pattern=[[1, NT]], base=0, channel_multiplier=0).then_inc(s_iota, 1)
            pool.iota(pidx_i[:, :], pattern=[[0, 1]], base=0, channel_multiplier=1).then_inc(s_iota, 1)
            pool.iota(tile_e_i[:, :], pattern=[[TG * P, NCH]], base=0, channel_multiplier=P).then_inc(s_iota, 1)
            pool.memset(acc0[:, :, :], 0.0).then_inc(s_acc0z, 1)
            def gather(table, w, row_len, free_sem, free_at):
                with pool.Fori(0, NBATCH // 2) as i:
                    for j in range(2 * K):
                        if j % K == 0:
                            s = j // K
                            pool.wait_ge(free_sem, free_at(i, s))
                            pool.sem_inc(s_turn, 1)
                            pool.tensor_copy(idx_now[:, j:j + K], idx[w][:, ds(i * 2 * K + j, K)]).then_inc(pool_own, 1)
                            pool.wait_ge(pool_own, i * 2 + (1 + s + w * NBATCH))
                            pool.sem_inc(s_turn, 1)
                        pool.indirect_dma_start(
                            G[:, j, 0:row_len], None, table,
                            bass.IndirectOffsetOnAxis(ap=idx_now[:, j:j + 1], axis=0),
                        ).then_inc(s_g[j], 16)

            pool.wait_ge(s_flag, 1)
            pool.wait_ge(s_key, 64)
            pool.wait_ge(s_firstc, 1)
            with pool.If(pool.value_load(sort_it[0:1, 0:1], min_val=0, max_val=1) < 1):
                for c in range(NCH):
                    for pad, tile in ((key_pad, keyT), (row_pad, rowT)):
                        pool.indirect_dma_start(tile[:, c, :], None, pad.rearrange("(n a) -> n a", a=1),
                                                bass.IndirectOffsetOnAxis(ap=first_i[:, c:c + 1], axis=0)
                                                ).then_inc(s_slices, 16)

            pool.wait_ge(s_top, 1)
            pool.partition_all_reduce(top_all[:, :], top[:, :], P, bass.bass_isa.ReduceOp.max).then_inc(s_topa, 1)

            pool.wait_ge(s_sorted[0], 1)
            pool.wait_ge(s_zout, 16 * NB)

            pool.wait_ge(s_spread, 1)
            with pool.If(pool.value_load(spread_it[0:1, 0:1], min_val=0, max_val=1) > 0):
                with pool.Fori(0, NT) as t:
                    pool.wait_ge(s_mfree, t + 1)
                    pool.sem_inc(s_turn, 1)
                    pool.tensor_copy(idx_now[:, 0:1], idx[0][:, ds(t, 1)]).then_inc(s_midx, 1)
                    pool.wait_ge(s_midx, t + 1)
                    pool.sem_inc(s_turn, 1)
                    pool.indirect_dma_start(
                        G[:, 0, :], None, z_table, bass.IndirectOffsetOnAxis(ap=idx_now[:, 0:1], axis=0),
                    ).then_inc(s_min, 16)
                pool.wait_ge(s_mfree, NT + 1)
                pool.sem_inc(s_turn, 1)

            gather(z_table, 0, ZW, s_msg, lambda i, s: i * 4 + (2 * s + 2))

            pool.wait_ge(s_bias, 16)
            pool.tensor_copy(acc1, bias_b[:, :].rearrange("p (a d) -> p a d", a=1).to_broadcast((P, NB, D))).then_inc(s_acc1z, 1)

            pool.wait_ge(s_sorted[1], 1)
            pool.wait_ge(s_xtout[0], 16 * (NB // 2 + 1))
            pool.wait_ge(s_xtout[1], 16 * (NB // 2))
            pool.wait_ge(s_msg, 4 + 2 * NBATCH)
            gather(xt_table, 1, D, s_agg1, lambda i, s: (i * 2 + (s + 1)) * K)

        def load_buckets(eng, name, w, t0):
            regs = [eng.alloc_register(f"bucket_{name}_{k}") for k in range(K)]
            eng.load(regs, bt[w][0:1, ds(t0, K)])
            return [eng.snap(r, donate=True, min_val=0, max_val=NB - 1) for r in regs]

        @block.vector
        def _(dve):
            own = Chain(dve, dve_own)
            V = nc.vector

            V.memset(pads[:, 0, :], NB * P)
            V.memset(pads[:, 1, :], 0).then_inc(s_padk, 1)
            V.memset(xs[:, NB - 1:NBP, :], 0.0).then_inc(s_xpad, 1)
            V.memset(attn_cols[:, :, :], 0.0).then_inc(s_azero, 1)
            V.memset(epst[:, :], EPS)
            V.memset(ones16[:, :], 1.0)
            V.memset(ones_f[:, :], 1.0)
            V.memset(zeros16[:, :], 0.0)
            for w in range(2):
                V.memset(lof[w][:, NT:NT + 2 * K], NO_NODE)
                own(V.memset(bt[w][:, NT:NT + K], 0))
            dve.wait_ge(s_iota, 3)
            V.tensor_copy(iota[:, :], iota_i[:, 0:P])
            V.tensor_copy(iota16[:, :], iota_i[:, :])
            V.tensor_copy(tile_e[:, :], tile_e_i[:, :])
            V.memset(step16[:, 0:1], -1.0)
            V.tensor_copy(step16[:, 1:NT + 1], iota_i[:, :])
            own(V.tensor_copy(pidx[:, :], pidx_i[:, :]))
            V.tensor_scalar(pidx_32[:, :], pidx[:, :], -32.0, None, ALU.add)
            for c in range(NCH):
                own(V.tensor_scalar(pidx_c[:, c:c + 1], pidx[:, :], float(c * CH), None, ALU.add))
            V.tensor_scalar(ident[:, :], iota[:, :], pidx[:, 0:1], None, ALU.is_equal)
            own(V.memset(base[:, :], 0.0))
            V.tensor_scalar(part_b[0:32, :], iota[0:32, 0:NB], pidx[0:32, 0:1], None, ALU.is_equal)
            V.tensor_scalar(part_b[32:32 + NB, :], iota[32:32 + NB, 0:NB], pidx_32[32:32 + NB, 0:1], None, ALU.is_equal)
            V.tensor_scalar(ident16[:, :], iota[:, :], pidx[:, 0:1], None, ALU.is_equal)
            V.tensor_scalar(before_p[:, :], iota[:, :], pidx[:, 0:1], None, ALU.is_gt)
            V.tensor_scalar(upto_p[:, :], iota[:, :], pidx[:, 0:1], None, ALU.is_ge)
            V.tensor_scalar(before_b[:, :], iota[:, :], pidx[:, 0:1], float(P), ALU.is_gt, ALU.mult)
            for c in range(NCH):
                last = V.tensor_scalar(before_t[:, c, :], iota16[:, 0:EC], pidx_c[:, c:c + 1], None, ALU.is_gt)
            own(last)
            V.sem_inc(s_const, 1)
            V.sem_inc(s_msg, 4)
            V.sem_inc(s_acc, 4)
            V.sem_inc(s_acc1, 8)
            V.sem_inc(s_xtd, 2)

            def variance(at):
                m_e, m_o = stats[:, at, 1], stats[:, at, 4]
                v_e, v_o = stats[:, at, 2], stats[:, at, 5]
                V.tensor_tensor(mean[:, at], m_e, m_o, ALU.add)
                V.tensor_tensor(half[:, at], m_e, m_o, ALU.subtract)
                own(V.tensor_tensor(var[:, at], v_e, v_o, ALU.add))
                own(V.tensor_tensor(half[:, at], half[:, at], half[:, at], ALU.mult))
                V.tensor_scalar(mean[:, at], mean[:, at], 0.5, None, ALU.mult)
                own(V.tensor_scalar(var[:, at], var[:, at], 1.0 / D, None, ALU.mult))
                V.scalar_tensor_tensor(var[:, at], half[:, at], 0.25, var[:, at], ALU.mult, ALU.add).then_inc(s_var, 1)

            def scale_and_shift(at, call):
                dve.wait_ge(s_std, call)
                own(V.reciprocal(rstd[:, at], rstd[:, at]))
                V.scalar_tensor_tensor(nmr[:, at], mean[:, at], -1.0, rstd[:, at], ALU.mult, ALU.mult).then_inc(s_ln, 1)


            a, b_ = ti[0:EP, 0:EC], tj[0:EP, 0:EC]

            def digits(w, link):
                key = e_dst if w == 0 else e_src
                if w == 0:
                    link(V.tensor_copy(a, e_src[:, :]))
                else:
                    link(V.tensor_scalar(a, e_typ[:, :], float(N), None, ALU.mult))
                    link(V.tensor_tensor(a, a, e_dst[:, :], ALU.add))
                link(V.tensor_scalar(b_, a, 4, None, ALU.logical_shift_right))
                V.tensor_copy(dig[w][:, 0, :], b_)
                link(V.tensor_scalar(a, a, 15, 7, ALU.bitwise_and, ALU.logical_shift_left))
                link(V.tensor_scalar(b_, key[:, :], P - 1, None, ALU.bitwise_and))
                link(V.tensor_tensor(a, a, b_, ALU.add))
                link(V.tensor_scalar(dig[w][:, 1, :], a, 1.0, None, ALU.add))

            def bucket_onehots(w):
                key = e_dst if w == 0 else e_src
                own(V.tensor_scalar(b_, key[:, :], 7, None, ALU.logical_shift_right))
                own(V.tensor_copy(hi16[:, :], b_))
                for b in range(NB):
                    last = V.tensor_scalar(onehot_b[0:EP, b, :], hi16[:, :], float(b), None, ALU.is_equal)
                last.then_inc(s_oh[w], 1)

            def tiles_of_buckets(w):
                dve.wait_ge(s_cnt[w], 1)
                V.tensor_copy(cntT[0:CH, :, :], bank[6][0:CH, 0:NCH * NB].rearrange("p (c b) -> p c b", b=NB)
                              ).then_inc(s_cntc[w], 1)
                dve.wait_ge(s_tot[w], 1)
                own(V.tensor_scalar(tiles_i[:, :], bank[7][0:NB, 0:1], float(P - 1), None, ALU.add))
                own(V.tensor_scalar(tiles_i[:, :], tiles_i[:, :], 7, None, ALU.logical_shift_right))
                own(V.tensor_scalar(tiles_s[:, :], tiles_i[:, :], float(-P), None, ALU.mult))
                V.tensor_tensor(short[:, :], bank[7][0:NB, 0:1], tiles_s[:, :], ALU.add)
                V.tensor_copy(tiles_f[:, :], tiles_i[:, :]).then_inc(s_tiles[w], 1)
                dve.wait_ge(s_incl[w], 1)
                own(V.tensor_copy(incl[:, :], bank[7][0:NB, 8:9]))
                V.tensor_scalar(passed[:, :], iota16[0:NB, :], incl[:, 0:1], None, ALU.is_ge).then_inc(s_passed[w], 1)
                dve.wait_ge(s_bt[w], 1)
                V.tensor_scalar(bt[w][:, 0:NT], bank[6][:, 0:NT], float(NB - 1), None, ALU.min).then_inc(s_btc[w], 1)

            def split_base(w, link):
                dve.wait_ge(s_base[w], 1)
                link(V.tensor_copy(base_i[:, :], bank[7][0:NB, 0:EC]))
                link(V.tensor_scalar(base_i[:, :], base_i[:, :], 5, 5, ALU.logical_shift_right, ALU.logical_shift_left))
                link(V.tensor_copy(base[0:NB, :], base_i[:, :]))
                V.tensor_tensor(base[32:32 + NB, :], bank[7][0:NB, 0:EC], base_i[:, :], ALU.subtract).then_inc(s_based[w], 1)

            def places(w, link):
                for b in range(NB):
                    dve.wait_ge(s_rank[w], b + 1)
                    if b:
                        dve.wait_ge(s_rankc[w], b)
                    V.copy_predicated(pos[:, :], onehot_b[0:EP, b, :].bitcast(u16),
                                      bank[RANK_BANKS[b % 4]][0:EP, 0:EC]).then_inc(s_rankc[w], 1)
                dve.wait_ge(s_rankc[w], NB)
                link(V.tensor_copy(a, pos[:, :]))
                link(V.tensor_scalar(b_, a, P - 1, None, ALU.bitwise_and))
                V.tensor_copy(plo[w][:, :], b_)
                link(V.tensor_scalar(a, a, 7, None, ALU.logical_shift_right))
                link(V.tensor_scalar(nphi[w][:, :], a, -1.0, 0.5, ALU.mult, ALU.add))

            def place_onehot(w, t, slot, g):
                if g == 0:
                    dve.wait_ge(s_hotu[w], t + 1)
                V.tensor_scalar(Ls[:, slot, g, :], iota16[0:EP, 0:P], plo[w][:, ds(t, 1)],
                                dig[w][:, g, ds(t, 1)], ALU.is_equal, ALU.mult).then_inc(s_L[w], 1)

            def bare_onehot(t, slot):
                dve.wait_ge(s_hotu[1], t + 1)
                V.tensor_scalar(Ls[:, slot, 0, :], iota16[0:EP, 0:P], plo[1][:, ds(t, 1)], None, ALU.is_equal).then_inc(s_L[1], 2)

            def sorted_tiles(w, banks, link):
                dve.wait_ge(s_srt[w], 1)
                for g in range(2):
                    link(V.tensor_copy(srt[:, g, :], bank[banks + g][:, 0:NT + 1]))
                for g in range(2):
                    link(V.tensor_tensor(srt[:, g, 0:NT], srt[:, g, 1:NT + 1], srt[:, g, 0:NT], ALU.subtract))
                link(V.tensor_scalar(srt[:, 1, 0:NT], srt[:, 1, 0:NT], 0.5, None, ALU.mult))
                link(V.tensor_scalar(ti[:, :], srt[:, 1, 0:NT], -1.0, 0.0, ALU.add, ALU.max))
                link(V.tensor_scalar(srt[:, 1, 0:NT], srt[:, 1, 0:NT], 0.0, NO_NODE, ALU.is_equal, ALU.mult))
                link(V.tensor_scalar(tj[:, :], ti[:, :], P - 1, None, ALU.bitwise_and))
                V.tensor_tensor(lof[w][:, 0:NT], srt[:, 1, 0:NT], tj[:, :], ALU.add)
                link(V.tensor_scalar(ti[:, :], ti[:, :], 7, None, ALU.logical_shift_right))
                link(V.scalar_tensor_tensor(idx[w][:, :], srt[:, 0, 0:NT], 8.0, ti[:, :], ALU.mult, ALU.add))

            dve.wait_ge(s_dst, 16)
            bucket_onehots(0)

            for c in range(XC):
                dve.wait_ge(s_x[c], 16)
                for b in range(c * (NB - 1) // XC, (c + 1) * (NB - 1) // XC):
                    V.bn_stats(row(stats, b), row(xs, b))
            dve.wait_ge(s_xlast, 16)
            for b in range(NB - 1, NBP):
                last = V.bn_stats(row(stats, b), row(xs, b))
            own(last)
            variance(slice(0, NBP))
            dve.wait_ge(s_keyn, 16)
            own(V.tensor_scalar(b_, e_nxt[:, :], 7, None, ALU.logical_shift_right))
            own(V.tensor_copy(hn16[:, :], b_))
            own(V.tensor_tensor(pos[:, :], hn16[:, :], hi16[:, :], ALU.is_lt))
            V.tensor_reduce(drops[:, :], pos[:, :], AX.X, ALU.add).then_inc(s_drop, 1)
            scale_and_shift(slice(0, NBP), 1)
            dve.wait_ge(s_wt, 1)
            own(V.tensor_copy(w0T[:, :, 0:D], bank[4][:, :].rearrange("p (j n) -> p j n", j=2)))
            V.tensor_copy(w0T[:, :, D:ZW], bank[5][:, 0:2 * 2 * H].rearrange("p (j n) -> p j n", j=2)).then_inc(s_wtc, 1)

            tiles_of_buckets(0)
            dve.wait_ge(s_dropc, 1)
            own(V.tensor_scalar(sort_it[:, :], bank[5][:, 0:1], 1.0, None, ALU.min))
            V.sem_inc(s_flag, 1)
            dve.wait_ge(s_first, 1)
            own(V.tensor_tensor(first_e[:, :], tile_e[:, :], bank[4][0:TG, 0:NCH], ALU.add))
            own(V.tensor_scalar(first_i[:, :], first_e[:, :], float(E), None, ALU.min))
            own(V.tensor_scalar(tile_b[:, :], bank[4][0:TG, 8:8 + NCH], float(NB - 1), float(P), ALU.min, ALU.mult))
            V.sem_inc(s_firstc, 1)

            sort_first = dve.value_load(sort_it[0:1, 0:1], min_val=0, max_val=1)
            with dve.If(sort_first > 0):
                slow = Chain(dve, slow_own)
                dve.wait_ge(s_edges, 32)
                digits(0, slow)
                V.sem_inc(s_sorting, 1)
                split_base(0, slow)
                places(0, slow)
                V.sem_inc(s_sorting, 1)
                with dve.Fori(0, EC // S) as i:
                    for k in range(S):
                        for g in range(2):
                            place_onehot(0, i * S + k, k, g)
                sorted_tiles(0, 4, slow)
            with dve.If(sort_first < 1):
                dve.wait_ge(s_slices, 16 * 2 * NCH)
                local = Chain(dve, slices_own)
                for c in range(NCH):
                    V.tensor_scalar(keyF[:, c, :], keyT[:, c, :], tile_b[:, c:c + 1], None, ALU.subtract)
                local(V.tensor_copy(rowF[:, :, :], rowT[:, :, :]))
                V.sem_inc(s_tl, 1)

            dve.wait_ge(s_edges, 32)
            digits(1, own)
            bucket_onehots(1)

            with dve.If(sort_first < 1):
                dve.wait_ge(s_tt, 1)
                turned = Chain(dve, turned_own)
                V.tensor_copy(lof[0][:, 0:NT], bank[4][:, 0:NT])
                turned(V.tensor_copy(idx[0][:, :], bank[5][:, 0:NT]))
            V.sem_inc(s_sorted[0], 1)

            dve.wait_ge(s_zc, NB + 2)
            V.tensor_copy(sdm[:, :, 0:H], zall[:, :, D + H:ZW])
            ss = zall[:, :, D:D + H].rearrange("p b h -> p h b")
            V.tensor_reduce(top[:, 0:H], ss, AX.X, ALU.max)
            own(V.tensor_reduce(top[:, H:2 * H], ss, AX.X, ALU.min))
            V.tensor_scalar(top[:, H:2 * H], top[:, H:2 * H], -1.0, None, ALU.mult).then_inc(s_top, 1)
            dve.wait_ge(s_topa, 1)
            own(V.tensor_tensor(spread[:, :], top_all[:, 0:H], top_all[:, H:2 * H], ALU.add))
            own(V.tensor_reduce(spread[:, 0:1], spread[:, :], AX.X, ALU.max))
            V.tensor_scalar(spread_it[:, :], spread[:, 0:1], MAX_SPREAD, None, ALU.is_gt).then_inc(s_spread, 1)
            own(V.tensor_tensor(tmp_m[:, :, :], zall[:, :, D + H:ZW],
                                top_all[:, 0:H].rearrange("p (a h) -> p a h", a=1).to_broadcast((P, NB, H)), ALU.add))
            own(V.scalar_tensor_tensor(sdm[:, :, H:2 * H], tmp_m[:, :, :], SLOPE, tmp_m[:, :, :], ALU.mult, ALU.max))

            dve.wait_ge(s_spread, 1)
            with dve.If(dve.value_load(spread_it[0:1, 0:1], min_val=0, max_val=1) > 0):
                own_max = Chain(dve, max_own)
                V.memset(OT[:, 0, :], 1.0)
                own_max(V.memset(tmp_m[:, :, :], NO_SCORE))
                V.sem_inc(s_mfree, 1)
                with dve.Fori(0, NT) as t:
                    own_max.enter(t, 4)
                    b = V.value_load(bt[0][0:1, ds(t, 1)], min_val=0, max_val=NB - 1)
                    V.tensor_scalar(O[:, 0, :], iota[:, :], lof[0][:, ds(t, 1)], None, ALU.is_equal)
                    dve.wait_ge(s_min, t * 16 + 16)
                    for h in range(H):
                        last = V.tensor_scalar(O[:, 1 + h, :], ident[:, :], G[:, 0, D + h:D + h + 1], None, ALU.mult)
                    last.then_inc(s_mdiag, 1)
                    dve.wait_ge(s_mspread, t + 1)
                    own_max(V.tensor_scalar(O[:, 5, :], bank[2][:, 0:P], -1.0, -NO_SCORE, ALU.add, ALU.mult))
                    own_max(V.tensor_tensor(O[:, 6:6 + H, :], bank[3][:, :].rearrange("p (h e) -> p h e", h=H),
                                            O[:, 5:6, :].to_broadcast((P, H, P)), ALU.add))
                    own_max(V.tensor_reduce(ev[:, 0, :], O[:, 6:6 + H, :], AX.X, ALU.max))
                    own_max(V.tensor_tensor(row(tmp_m, b), row(tmp_m, b), ev[:, 0, :], ALU.max))
                    V.sem_inc(s_mfree, 1)
                    own_max.leave(4, NT)
                own_max(V.tensor_tensor(tmp_m[:, :, :], tmp_m[:, :, :], sdm[:, :, 0:H], ALU.add))
                own_max(V.scalar_tensor_tensor(sdm[:, :, H:2 * H], tmp_m[:, :, :], SLOPE, tmp_m[:, :, :], ALU.mult, ALU.max))
            V.sem_inc(s_sdm, 1)

            def onehots(w, t0, into, n=K):
                return V.tensor_tensor(into, iota[:, :].rearrange("p (a n) -> p a n", a=1).to_broadcast((P, n, P)),
                                       lof[w][:, ds(t0, n)].rearrange("p (k a) -> p k a", a=1).to_broadcast((P, n, P)),
                                       ALU.is_equal)

            dve.wait_ge(s_acc0z, 1)
            onehots(0, 0, Ob[:, :, :]).then_inc(s_O, 1)

            tiles_of_buckets(1)
            split_base(1, own)
            dve.wait_ge(s_Ot, 1)
            dve.wait_ge(s_O32, 1)
            onehots(0, K, Ob[:, :, :]).then_inc(s_O, 1)
            places(1, own)

            with dve.Fori(0, NBATCH // 2) as i:
                own.enter(i, 6)
                for s in range(2):
                    t0 = i * 2 * K + s * K
                    g = G[:, s * K:(s + 1) * K, :]
                    scores = bank[1][:, 0:K * 2 * H].rearrange("p (k c) -> p k c", k=K)
                    dve.wait_ge(s_sd, i * 2 + (s + 1))
                    for j in range(K):
                        dve.wait_ge(s_g[s * K + j], i * 16 + 16)
                    own(V.tensor_tensor(ev[:, :, :], g[:, :, D:D + H], scores[:, :, 0:H], ALU.add))
                    own(V.scalar_tensor_tensor(ev2[:, :, :], ev[:, :, :], SLOPE, ev[:, :, :], ALU.mult, ALU.max))
                    own(V.tensor_tensor(ev[:, :, :], ev2[:, :, :], scores[:, :, H:2 * H], ALU.subtract))
                    V.tensor_scalar(ev[:, :, :], ev[:, :, :], 0.0, None, ALU.min).then_inc(s_ev, 1)
                    for c in range(2):
                        bare_onehot(i * 2 * C0 + (s * C0 + c), s * C0 + c)
                    dve.wait_ge(s_ex, i * 2 + (s + 1))
                    for q in range(2):
                        ks = slice(q * K // 2, (q + 1) * K // 2)
                        V.tensor_tensor(msg[:, ks, 0:D].rearrange("p k (h d) -> p k h d", h=H),
                                        g[:, ks, 0:D].rearrange("p k (h d) -> p k h d", h=H),
                                        msg[:, ks, D:MW].rearrange("p k (h a) -> p k h a", a=1).to_broadcast((P, K // 2, H, DH)),
                                        ALU.mult).then_inc(s_msg, 1)
                    buckets_of = load_buckets(dve, f"dve0{s}", 0, t0)
                    for k in range(K):
                        b = buckets_of[k]
                        dve.wait_ge(s_agg, t0 + (k + 1))
                        dve.wait_ge(s_acc, t0 + (k + 4))
                        V.tensor_tensor(row(acc0, b), row(acc0, b), bank[2 + k % 4][:, 0:MW], ALU.add).then_inc(s_acc, 1)
                        if k in (0, 2):
                            c = 2 + k // 2
                            bare_onehot(i * 2 * C0 + (s * C0 + c), s * C0 + c)
                        if k >= K - 2:
                            place_onehot(1, i * 2 * C0 + (s * C0 + 4), s * C0 + 4, k - (K - 2))
                        if k == 1:
                            dve.wait_ge(s_Ot, i * 2 + (s + 2))
                            dve.wait_ge(s_O32, i * 2 + (s + 2))
                        if k in (1, 3, 4, 5):
                            q = (1, 3, 4, 5).index(k) * 2
                            last = onehots(0, t0 + (2 * K + q), Ob[:, q:q + 2, :], 2)
                            if q == K - 2:
                                last.then_inc(s_O, 1)
                own.leave(6, NBATCH // 2)

            dve.wait_ge(s_acc, NT + 4)
            own(V.tensor_scalar(rden[:, :, :], acc0[:, :, D:MW], 1e-9, None, ALU.max))
            own(V.reciprocal(rden[:, :, :], rden[:, :, :]))

            def pair_variance(first):
                at = ds(first, 2)
                q = acc0[:, at, 0:D].rearrange("p b (h d) -> p b h d", h=H)
                own(V.tensor_tensor(q, q, rden[:, at, :].rearrange("p b (h a) -> p b h a", a=1).to_broadcast((P, 2, H, DH)), ALU.mult))
                own(V.tensor_tensor(xs[:, at, :], xs[:, at, :], acc0[:, at, 0:D], ALU.add))
                for u in range(2):
                    own(V.bn_stats(row(stats, first + u), row(xs, first + u)))
                variance(at)
            pair_variance(0)
            scale_and_shift(ds(0, 2), 2)

            def copy_hT(b, u, i):
                dve.wait_ge(s_hT, b + (NB + 3))
                V.tensor_copy(hT[:, u, :, :].rearrange("p j n -> p (j n)"), bank[u][:, 0:D]).then_inc(s_hTc, 1)

            def place_onehots(b, u, n):
                for k in range(n):
                    for g in range(2):
                        place_onehot(1, b * C1 + (C0 * NBATCH + k), (u * C1 + k) % S, g)

            def copy_xt(b, u, i):
                dve.wait_ge(s_stage, b + 1)
                for c in range(2):
                    dve.wait_ge(s_xt, b * 4 + (c + 3))
                    V.tensor_copy(stage[:, u, (c + 2) * 512:(c + 3) * 512], bank[4 + c][:, :]).then_inc(s_xtd, 1)
            with dve.Fori(0, NB // 2) as i:
                own.enter(i, 8)
                for u in range(2):
                    copy_hT(i * 2 + u, u, i)
                place_onehots(i * 2, 0, C1)
                copy_xt(i * 2, 0, i)
                pair_variance(i * 2 + 2)
                place_onehots(i * 2 + 1, 1, C1)
                scale_and_shift(ds(i * 2 + 2, 2), i + 3)
                copy_xt(i * 2 + 1, 1, i)
                own.leave(8, NB // 2)
            copy_hT(NB - 1, 0, NB // 2)
            place_onehots(NB - 1, 0, CL)
            sorted_tiles(1, 6, own)
            copy_xt(NB - 1, 0, NB // 2)
            V.sem_inc(s_sorted[1], 1)

            dve.wait_ge(s_acc1z, 1)
            onehots(1, 0, O[:, 0:K, :]).then_inc(s_O1, 1)
            with dve.Fori(0, NBATCH // 2) as i:
                for s in range(2):
                    t0 = i * 2 * K + s * K
                    onehots(1, t0 + K, O[:, (1 - s) * K:(2 - s) * K, :]).then_inc(s_O1, 1)
                    buckets_of = load_buckets(dve, f"dve1{s}", 1, t0)
                    for k in range(K):
                        b = buckets_of[k]
                        dve.wait_ge(s_agg1, t0 + (k + 1 + 2 * K))
                        dve.wait_ge(s_acc1, t0 + (k + 8))
                        r = acc1[:, ds(b, 1), :].rearrange("p b d -> p (b d)")
                        V.tensor_tensor(r, r, bank[k][:, 0:D], ALU.add).then_inc(s_acc1, 1)

            dve.wait_ge(s_acc1, NT + 8)
            with dve.Fori(0, NB // FC) as c:
                r = acc1[:, ds(c * FC, FC), :]
                q = xs[:, ds(c * FC, FC), :]
                V.scalar_tensor_tensor(q, r, 0.0, q, ALU.max, ALU.add).then_inc(s_fin, 1)

        @block.scalar
        def _(act):
            A = nc.scalar
            A.sem_inc(s_xta, 2)
            A.sem_inc(s_zc, 2)

            def deviation(at, call):
                act.wait_ge(s_var, call)
                A.activation(rstd[:, at], var[:, at], ACT.Sqrt, bias=epst[:, 0:1]).then_inc(s_std, 1)

            def make_h(base):
                def one(b, u, i):
                    act.wait_ge(s_hT, b + (base + 1))
                    A.activation(hn[:, u, :], row(xs, b), ACT.Relu, bias=nmr[:, ds(b, 1)], scale=rstd[:, ds(b, 1)]
                                 ).then_inc(s_h, 1)
                return one

            def tile_step(w, t, slot):
                act.wait_ge(s_hotu[w], t + 1)
                A.activation(Hs[:, slot, 0:NT + 1], step16[0:EP, :], ACT.Sign, bias=nphi[w][:, ds(t, 1)]).then_inc(s_H[w], 1)

            def times_digits(t, slot):
                act.wait_ge(s_L[1], t * 2 + 2)
                for g in (1, 0):
                    A.mul(Ls[:, slot, g, :], Ls[:, slot, 0, :], dig[1][:, g, ds(t, 1)])

            act.wait_ge(s_const, 1)
            deviation(slice(0, NBP), 1)
            act.wait_ge(s_ln, 1)

            def copy_hT(b, u, i):
                act.wait_ge(s_hT, b + 3)
                A.copy(hT[:, u, :, :].rearrange("p j n -> p (j n)"), bank[u][:, 0:D]).then_inc(s_hTc, 1)

            def copy_z(b, u, i):
                act.wait_ge(s_z, b + 1)
                A.copy(row(zall, b), bank[2 + u][:, 0:ZW]).then_inc(s_zc, 1)
            first_h = make_h(0)
            for u in range(2):
                first_h(u, u, 0)
            with act.Fori(0, NB // 2) as i:
                for u in range(2):
                    copy_hT(i * 2 + u, u, i)
                for u in range(2):
                    first_h(i * 2 + 2 + u, u, i)
                for u in range(2):
                    copy_z(i * 2 + u, u, i)
            copy_hT(NB - 1, 0, NB // 2)
            copy_z(NB - 1, 0, NB // 2)

            act.wait_ge(s_flag, 1)
            with act.If(act.value_load(sort_it[0:1, 0:1], min_val=0, max_val=1) > 0):
                act.wait_ge(s_sorting, 2)
                with act.Fori(0, EC // S) as i:
                    for k in range(S):
                        tile_step(0, i * S + k, k)

            def turned(batch, half_):
                act.wait_ge(s_O, batch + 1)
                A.copy(O[:, half_ * K:(half_ + 1) * K, :].rearrange("p k n -> p (k n)"),
                       Ob[:, :, :].rearrange("p k n -> p (k n)")).then_inc(s_O32, 1)
                act.wait_ge(s_Ot, batch + 1)
                A.copy(OT[:, :, :].rearrange("p k e -> p (k e)"), bank[0][:, :].bitcast(bf16)).then_inc(s_OTc, 1)
            turned(0, 0)
            with act.Fori(0, NBATCH // 2) as i:
                for s in range(2):
                    act.wait_ge(s_ev, i * 2 + (s + 1))
                    A.activation(msg[:, :, D:MW], ev[:, :, :], ACT.Exp).then_inc(s_ex, 1)
                    turned(i * 2 + (s + 1), 1 - s)
                    for c in range(C0):
                        if c < 4:
                            times_digits(i * 2 * C0 + (s * C0 + c), s * C0 + c)
                        tile_step(1, i * 2 * C0 + (s * C0 + c), s * C0 + c)

            deviation(ds(0, 2), 2)
            next_h = make_h(NB)

            def copy_xt(b, u, i):
                act.wait_ge(s_stage, b + 1)
                for k in range(CL if isinstance(b, int) else C1):
                    tile_step(1, b * C1 + (C0 * NBATCH + k), (u * C1 + k) % S)
                for c in range(2):
                    act.wait_ge(s_xt, b * 4 + (c + 1))
                    A.copy(stage[:, u, c * 512:(c + 1) * 512], bank[2 + c][:, :]).then_inc(s_xta, 1)
            with act.Fori(0, NB // 2) as i:
                act.wait_ge(s_ln, i + 2)
                for u in range(2):
                    next_h(i * 2 + u, u, i)
                for u in range(2):
                    copy_xt(i * 2 + u, u, i)
                deviation(ds(i * 2 + 2, 2), i + 3)
            act.wait_ge(s_ln, NB // 2 + 2)
            next_h(NB - 1, 0, NB // 2)
            copy_xt(NB - 1, 0, NB // 2)

        @block.tensor
        def _(pe):
            T = nc.tensor
            T.sem_inc(s_hT, 2)
            T.sem_inc(s_hTc, 2)
            for w in range(2):
                T.sem_inc(s_hotu[w], S)
            T.sem_inc(s_agg1, 2 * K)
            def edges_of_buckets(w):
                pe.wait_ge(s_oh[w], 1)
                for c in range(NCH):
                    for b in range(NB):
                        last = T.matmul(bank[6][0:CH, c * NB + b:c * NB + b + 1], onehot_b[0:EP, b, c * CH:(c + 1) * CH],
                                        ones16[0:EP, 0:1], start=True, stop=True)
                last.then_inc(s_cnt[w], 1)

            pe.wait_ge(s_const, 1)
            edges_of_buckets(0)
            pe.wait_ge(s_w0, 16)
            pe.wait_ge(s_attn, 16 * 8)
            for k in range(2):
                for j in range(2):
                    T.transpose(bank[4][:, (k * 2 + j) * P:(k * 2 + j + 1) * P], w_rows[:, j, k * P:(k + 1) * P], ident[:, :])
            for k in range(2):
                for j in range(2):
                    last = T.matmul(bank[5][:, k * 2 * H:(k + 1) * 2 * H], w_rows[:, j, k * P:(k + 1) * P],
                                    attn_cols[:, j, :], start=(j == 0), stop=(j == 1))
            last.then_inc(s_wt, 1)

            def turn_h(base):
                def one(b, u, i):
                    pe.wait_ge(s_h, b + (base + base // NB + 1))
                    pe.wait_ge(s_hTc, b + (base + 1))
                    for j in range(2):
                        last = T.transpose(bank[u][:, j * P:(j + 1) * P], hn[:, u, j * P:(j + 1) * P], ident[:, :])
                    last.then_inc(s_hT, 1)
                return one

            def layer0_table(b, u, i):
                pe.wait_ge(s_hTc, b + 3)
                pe.wait_ge(s_zc, b + 1)
                for j in range(2):
                    last = T.matmul(bank[2 + u][:, 0:ZW], hT[:, u, j, :], w0T[:, j, :], start=(j == 0), stop=(j == 1))
                last.then_inc(s_z, 1)

            def tiles_of_buckets(w):
                pe.wait_ge(s_cntc[w], 1)
                for c in range(NCH):
                    last = T.matmul(bank[7][0:NB, 0:1], cntT[0:CH, c, :], ones16[0:CH, 0:1], start=(c == 0), stop=(c == NCH - 1))
                last.then_inc(s_tot[w], 1)
                pe.wait_ge(s_tiles[w], 1)
                T.matmul(bank[7][0:NB, 8:9], upto_p[0:NB, 0:NB], tiles_f[:, :], start=True, stop=True).then_inc(s_incl[w], 1)
                pe.wait_ge(s_passed[w], 1)
                T.matmul(bank[6][:, 0:NT], ones16[0:NB, :], passed[:, :], start=True, stop=True).then_inc(s_bt[w], 1)

            def columns_before(w):
                T.matmul(bank[7][0:NB, 0:EC], before_b[0:NB, 0:NB], tiles_f[:, 0:1].to_broadcast((NB, EC)), start=True, stop=False)
                for c in range(NCH):
                    last = T.matmul(bank[7][0:NB, 0:EC], cntT[0:CH, c, :], before_t[0:CH, c, :], start=False, stop=(c == NCH - 1))
                last.then_inc(s_base[w], 1)

            def places(w):
                pe.wait_ge(s_zc, NB + 2)
                pe.wait_ge(s_based[w], 1)
                for b in range(NB):
                    if b >= 4:
                        pe.wait_ge(s_rankc[w], b - 3)
                    o = bank[RANK_BANKS[b % 4]][0:EP, 0:EC]
                    T.matmul(o, before_p[0:EP, 0:EP], onehot_b[0:EP, b, :], start=True, stop=False)
                    T.matmul(o, part_b[:, b:b + 1].to_broadcast((32 + NB, EP)), base[:, :], start=False,
                             stop=True).then_inc(s_rank[w], 1)

            def open_sums(banks):
                for g in range(2):
                    T.matmul(bank[banks + g][:, 0:NT + 1], zeros16[0:EP, 0:P], zeros16[0:EP, :], start=True, stop=False)

            def sort_column(w, banks, t, slot):
                pe.wait_ge(s_L[w], t * 2 + 2)
                pe.wait_ge(s_H[w], t + 1)
                for g in range(2):
                    last = T.matmul(bank[banks + g][:, 0:NT + 1], Ls[:, slot, g, :], Hs[:, slot, 0:NT + 1], start=False, stop=False)
                last.then_inc(s_hotu[w], 1)

            def close_sums(banks, w):
                for g in range(2):
                    last = T.matmul(bank[banks + g][:, 0:NT + 1], zeros16[0:EP, 0:P], zeros16[0:EP, :], start=False, stop=True)
                last.then_inc(s_srt[w], 1)

            pe.wait_ge(s_drop, 1)
            pe.wait_ge(s_wtc, 1)
            T.matmul(bank[5][:, 0:1], ones_f[:, :], drops[:, :], start=True, stop=True).then_inc(s_dropc, 1)
            tiles_of_buckets(0)
            for c in range(NCH):
                T.matmul(bank[4][0:TG, c:c + 1], passed[:, c * TG:(c + 1) * TG], short[:, :], start=True, stop=True)
                last = T.matmul(bank[4][0:TG, 8 + c:9 + c], passed[:, c * TG:(c + 1) * TG], ones16[0:NB, 0:1],
                                start=True, stop=True)
            last.then_inc(s_first, 1)

            pe.wait_ge(s_wtc, 1)
            buckets(pe, turn_h(0), layer0_table)

            pe.wait_ge(s_flag, 1)
            pe.wait_ge(s_firstc, 1)
            sort_first = pe.value_load(sort_it[0:1, 0:1], min_val=0, max_val=1)
            with pe.If(sort_first > 0):
                pe.wait_ge(s_sorting, 1)
                columns_before(0)
                places(0)
                pe.wait_ge(s_rankc[0], NB)
                open_sums(4)
                with pe.Fori(0, EC // S) as i:
                    for k in range(S):
                        sort_column(0, 4, i * S + k, k)
                close_sums(4, 0)
            with pe.If(sort_first < 1):
                pe.wait_ge(s_tl, 1)
                for c in range(NCH):
                    T.transpose(bank[4][:, c * TG:(c + 1) * TG], keyF[:, c, :], ident[0:TG, 0:TG])
                    last = T.transpose(bank[5][:, c * TG:(c + 1) * TG], rowF[:, c, :], ident[0:TG, 0:TG])
                last.then_inc(s_tt, 1)
            edges_of_buckets(1)

            def turn_onehots(batch):
                pe.wait_ge(s_O, batch + 1)
                for k in range(K):
                    last = T.transpose(bank[0][:, :].bitcast(bf16)[:, k * P:(k + 1) * P], Ob[:, k, :], ident16[:, :])
                last.then_inc(s_Ot, 1)

            def scores(name, batch, t0):
                buckets_of = load_buckets(pe, f"pe{name}", 0, t0)
                pe.wait_ge(s_OTc, batch + 1)
                for k in range(K):
                    last = T.matmul(bank[1][:, k * 2 * H:(k + 1) * 2 * H], OT[:, k, :], row(sdm, buckets_of[k]),
                                    start=True, stop=True)
                last.then_inc(s_sd, 1)

            pe.wait_ge(s_spread, 1)
            with pe.If(pe.value_load(spread_it[0:1, 0:1], min_val=0, max_val=1) > 0):
                with pe.Fori(0, NT) as t:
                    pe.wait_ge(s_mdiag, t + 1)
                    T.transpose(bank[2][:, 0:P], O[:, 0, :], ident[:, :])
                    T.matmul(bank[3][:, :], OT[:, 0, :], O[:, 1:1 + H, :].rearrange("p h e -> p (h e)"),
                             start=True, stop=True).then_inc(s_mspread, 1)

            pe.wait_ge(s_btc[0], 1)
            pe.wait_ge(s_sdm, 1)
            turn_onehots(0)
            tiles_of_buckets(1)
            columns_before(1)
            scores("first", 0, 0)

            pe.wait_ge(s_sorted[0], 1)
            places(1)
            pe.wait_ge(s_rankc[1], NB)
            open_sums(6)
            with pe.Fori(0, NBATCH // 2) as i:
                for s in range(2):
                    t0 = i * 2 * K + s * K
                    turn_onehots(i * 2 + (s + 1))
                    pe.wait_ge(s_O32, i * 2 + (s + 1))
                    for k in range(K):
                        if k % 4 == 0:
                            pe.wait_ge(s_msg, i * 4 + (2 * s + k // 4 + 5))
                        pe.wait_ge(s_acc, t0 + (k + 1))
                        T.matmul(bank[2 + k % 4][:, 0:MW], O[:, s * K + k, :], msg[:, k, :], start=True, stop=True).then_inc(s_agg, 1)
                    pe.wait_ge(s_ev, i * 2 + (s + 1))
                    scores(s, i * 2 + (s + 1), t0 + K)
                    for c in range(C0):
                        sort_column(1, 6, i * 2 * C0 + (s * C0 + c), s * C0 + c)

            pe.wait_ge(s_w1, 32)
            def columns_with(b, u, n):
                for k in range(n):
                    sort_column(1, 6, b * C1 + (C0 * NBATCH + k), (u * C1 + k) % S)

            def layer1_table(b, u, i):
                if isinstance(b, int):
                    columns_with(b, u, CL)
                    close_sums(6, 1)
                pe.wait_ge(s_hTc, b + (NB + 3))
                for c in range(4):
                    pe.wait_ge(s_xta if c < 2 else s_xtd, b * 2 + (c % 2 + 1))
                    for q in range(2):
                        for j in range(2):
                            last = T.matmul(bank[2 + c][:, q * D:(q + 1) * D], hT[:, u, j, :], w1s[:, j, 2 * c + q, :],
                                            start=(j == 0), stop=(j == 1))
                    last.then_inc(s_xt, 1)
                if not isinstance(b, int):
                    columns_with(b, u, C1)
            buckets(pe, turn_h(NB), layer1_table)
            pe.wait_ge(s_sorted[1], 1)

            with pe.Fori(0, NBATCH // 2) as i:
                for s in range(2):
                    t0 = i * 2 * K + s * K
                    pe.wait_ge(s_O1, i * 2 + (s + 1))
                    for k in range(K):
                        pe.wait_ge(s_g[s * K + k], i * 16 + 16 * (NBATCH // 2 + 1))
                        pe.wait_ge(s_acc1, t0 + (k + 1))
                        T.matmul(bank[k][:, 0:D], O[:, s * K + k, :], G[:, s * K + k, 0:D], start=True, stop=True).then_inc(s_agg1, 1)


_INS = ['x', 'src', 'dst', 'edge_type_8', 'L0_gnn_W', 'L0_gnn_attn', 'L1_gnn_weight', 'L1_gnn_bias']
_OUTS = [((N, D), 'float32')]


def kernel(**inputs):
    import numpy as _np
    import concourse.bacc as _bacc
    from concourse import mybir as _mybir
    from concourse.bass_utils import run_bass_kernel_spmd as _run

    nc = _bacc.Bacc("TRN2", target_bir_lowering=False, num_devices=1)
    arrays, args = {}, []
    for name in _INS:
        a = _np.ascontiguousarray(inputs[name])
        arrays[f"in_{name}_dram"] = a
        args.append(nc.dram_tensor(f"in_{name}_dram", a.shape, _mybir.dt.from_np(a.dtype), kind="ExternalInput").ap())
    for i, (shape, dtype) in enumerate(_OUTS):
        dt = _mybir.dt.from_np(_np.dtype(dtype))
        args.append(nc.dram_tensor(f"out_{i}_dram", shape, dt, kind="ExternalOutput").ap())
    build(nc, *args)
    r = _run(nc, [arrays], core_ids=[0])
    return r.results[0]["out_0_dram"]
```
